# Optimizing a Trainium2 kernel written in Bass

```python
import numpy as np
import jax
import jax.numpy as jnp

def _softmax(x, axis=-1):
    return jax.nn.softmax(x, axis=axis)

def _gelu(x):
    return jax.nn.gelu(x, approximate=True)

def _silu(x):
    return jax.nn.silu(x)

def _sigmoid(x):
    return jax.nn.sigmoid(x)

def _layernorm(x, axis=-1, eps=1e-05):
    m = jnp.mean(x, axis=axis, keepdims=True)
    v = jnp.var(x, axis=axis, keepdims=True)
    return (x - m) / jnp.sqrt(v + eps)

def _scatter_add(tgt, idx, src, axis=0):
    return tgt.at[idx].add(src)

def _segment_sum(src, seg, n):
    return jax.ops.segment_sum(src, seg, n)
kernel_name = 'mk_audio_tower_d1_tok_audfeat512_r4_81dd2d'

def setup_inputs(seed: int=0):
    np.random.seed(seed)
    _w = jnp.asarray

    def _rec_inputs():
        import jax
        import jax.numpy as jnp
        _rk = jax.random.key(seed)
        x = -0.000153849 + 1.00027 * jax.random.normal(jax.random.fold_in(_rk, 1), (32, 125, 24), jnp.float32)
        return x
    x = _rec_inputs()

    def _L0_tok_setup():
        import jax, jax.numpy as jnp
        import numpy as np
        CONTEXT = 5
        DILATION = 1
        BN_EPS = 1e-05
        key = jax.random.key(seed)
        k1, k2 = jax.random.split(key)
        B, T, D = (64, 1024, 24)
        OUT = 128
        x = jax.random.normal(k1, (B, T, D), dtype=jnp.float32)
        W = jax.random.normal(k2, (OUT, CONTEXT * D), dtype=jnp.float32) * 0.05
        b = jnp.zeros((OUT,), dtype=jnp.float32)
        gamma = jnp.ones((OUT,), dtype=jnp.float32)
        beta = jnp.zeros((OUT,), dtype=jnp.float32)
        return {'x': x, 'W': W, 'b': b, 'gamma': gamma, 'beta': beta}
    _L0_tok_all = _L0_tok_setup()
    _L0_tok_in = {k: v for k, v in _L0_tok_all.items() if k in ('W', 'b', 'gamma', 'beta')}
    del _L0_tok_all

    def _L0_attn_setup():
        import jax, jax.numpy as jnp
        import numpy as np
        D_MODEL = 128
        N_HEADS = 8
        D_HEAD = D_MODEL // N_HEADS
        EPS = 1e-06

        def _split_heads(t, B, S):
            return t.reshape(B, S, N_HEADS, D_HEAD).transpose(0, 2, 1, 3)

        def _reference_tuple_inner(x, Wq, bq, Wk, bk, Wv, bv, Wo, bo):
            B, S, _ = x.shape
            q = _split_heads(x @ Wq.T + bq, B, S)
            k = _split_heads(x @ Wk.T + bk, B, S)
            v = _split_heads(x @ Wv.T + bv, B, S)
            q = jax.nn.relu(q)
            k = jax.nn.relu(k)
            k_sum = k.sum(axis=-1, keepdims=True)
            attn = jnp.einsum('bhnd,bhmd->bhnm', q, k) / (k_sum + EPS)
            attn = jax.nn.softmax(attn, axis=-1)
            out = jnp.einsum('bhnm,bhmd->bhnd', attn, v)
            out = out.transpose(0, 2, 1, 3).reshape(B, S, D_MODEL)
            return (out @ Wo.T + bo, attn)
        key = jax.random.key(seed)
        ks = jax.random.split(key, 9)
        B, S = (2, 512)
        scale = 0.02
        x = jax.random.normal(ks[0], (B, S, D_MODEL), dtype=jnp.float32)
        Wq = jax.random.normal(ks[1], (D_MODEL, D_MODEL), dtype=jnp.float32) * scale
        Wk = jax.random.normal(ks[2], (D_MODEL, D_MODEL), dtype=jnp.float32) * scale
        Wv = jax.random.normal(ks[3], (D_MODEL, D_MODEL), dtype=jnp.float32) * scale
        Wo = jax.random.normal(ks[4], (D_MODEL, D_MODEL), dtype=jnp.float32) * scale
        bq = jax.random.normal(ks[5], (D_MODEL,), dtype=jnp.float32) * scale
        bk = jax.random.normal(ks[6], (D_MODEL,), dtype=jnp.float32) * scale
        bv = jax.random.normal(ks[7], (D_MODEL,), dtype=jnp.float32) * scale
        bo = jax.random.normal(ks[8], (D_MODEL,), dtype=jnp.float32) * scale
        return {'x': x, 'Wq': Wq, 'bq': bq, 'Wk': Wk, 'bk': bk, 'Wv': Wv, 'bv': bv, 'Wo': Wo, 'bo': bo}
    _L0_attn_all = _L0_attn_setup()
    _L0_attn_in = {k: v for k, v in _L0_attn_all.items() if k in ('Wq', 'bq', 'Wk', 'bk', 'Wv', 'bv', 'Wo', 'bo')}
    del _L0_attn_all

    def _L0_ffn_setup():
        import jax, jax.numpy as jnp
        import numpy as np
        H = 128
        F = 512
        E = 16
        SHARED = 2
        TOP_K = 4
        B, S = (2, 512)

        def _mlp(x, w1, b1, w2, b2):
            return jax.nn.gelu(x @ w1 + b1, approximate=False) @ w2 + b2
        key = jax.random.key(seed)
        ks = jax.random.split(key, 10)
        sc = 0.02
        return {'hidden_states': jax.random.normal(ks[0], (B, S, H), dtype=jnp.float32), 'gate_w': jax.random.normal(ks[1], (E, H), dtype=jnp.float32) * sc, 're_w1': jax.random.normal(ks[2], (E, H, F), dtype=jnp.float32) * sc, 're_b1': jnp.zeros((E, F), dtype=jnp.float32), 're_w2': jax.random.normal(ks[3], (E, F, H), dtype=jnp.float32) * sc, 're_b2': jnp.zeros((E, H), dtype=jnp.float32), 'se_w1': jax.random.normal(ks[4], (SHARED, H, F), dtype=jnp.float32) * sc, 'se_b1': jnp.zeros((SHARED, F), dtype=jnp.float32), 'se_w2': jax.random.normal(ks[5], (SHARED, F, H), dtype=jnp.float32) * sc, 'se_b2': jnp.zeros((SHARED, H), dtype=jnp.float32)}
    _L0_ffn_all = _L0_ffn_setup()
    _L0_ffn_in = {k: v for k, v in _L0_ffn_all.items() if k in ('gate_w', 're_w1', 're_b1', 're_w2', 're_b2', 'se_w1', 'se_b1', 'se_w2', 'se_b2')}
    del _L0_ffn_all
    return {'x': x, 'L0_tok_W': _L0_tok_in['W'], 'L0_tok_b': _L0_tok_in['b'], 'L0_tok_gamma': _L0_tok_in['gamma'], 'L0_tok_beta': _L0_tok_in['beta'], 'L0_attn_Wq': _L0_attn_in['Wq'], 'L0_attn_bq': _L0_attn_in['bq'], 'L0_attn_Wk': _L0_attn_in['Wk'], 'L0_attn_bk': _L0_attn_in['bk'], 'L0_attn_Wv': _L0_attn_in['Wv'], 'L0_attn_bv': _L0_attn_in['bv'], 'L0_attn_Wo': _L0_attn_in['Wo'], 'L0_attn_bo': _L0_attn_in['bo'], 'L0_ffn_gate_w': _L0_ffn_in['gate_w'], 'L0_ffn_re_w1': _L0_ffn_in['re_w1'], 'L0_ffn_re_b1': _L0_ffn_in['re_b1'], 'L0_ffn_re_w2': _L0_ffn_in['re_w2'], 'L0_ffn_re_b2': _L0_ffn_in['re_b2'], 'L0_ffn_se_w1': _L0_ffn_in['se_w1'], 'L0_ffn_se_b1': _L0_ffn_in['se_b1'], 'L0_ffn_se_w2': _L0_ffn_in['se_w2'], 'L0_ffn_se_b2': _L0_ffn_in['se_b2']}

def reference(x, L0_tok_W, L0_tok_b, L0_tok_gamma, L0_tok_beta, L0_attn_Wq, L0_attn_bq, L0_attn_Wk, L0_attn_bk, L0_attn_Wv, L0_attn_bv, L0_attn_Wo, L0_attn_bo, L0_ffn_gate_w, L0_ffn_re_w1, L0_ffn_re_b1, L0_ffn_re_w2, L0_ffn_re_b2, L0_ffn_se_w1, L0_ffn_se_b1, L0_ffn_se_w2, L0_ffn_se_b2):
    import jax
    import jax.numpy as jnp

    def _L0_tok_ref(x, W, b, gamma, beta):
        import jax, jax.numpy as jnp
        import numpy as np
        CONTEXT = 5
        DILATION = 1
        BN_EPS = 1e-05
        B, T, D = x.shape
        Tp = T - DILATION * (CONTEXT - 1)
        frames = jnp.concatenate([x[:, i * DILATION:i * DILATION + Tp, :] for i in range(CONTEXT)], axis=-1)
        h = jax.nn.relu(jnp.einsum('btf,of->bto', frames, W) + b)
        mean = jnp.mean(h, axis=(0, 1))
        var = jnp.mean(jnp.square(h - mean), axis=(0, 1))
        y = gamma * (h - mean) * jax.lax.rsqrt(var + BN_EPS) + beta
        return y

    def _L0_attn_ref(x, Wq, bq, Wk, bk, Wv, bv, Wo, bo):
        import jax, jax.numpy as jnp
        import numpy as np
        D_MODEL = 128
        N_HEADS = 8
        D_HEAD = D_MODEL // N_HEADS
        EPS = 1e-06

        def _split_heads(t, B, S):
            return t.reshape(B, S, N_HEADS, D_HEAD).transpose(0, 2, 1, 3)

        def _reference_tuple_inner(x, Wq, bq, Wk, bk, Wv, bv, Wo, bo):
            B, S, _ = x.shape
            q = _split_heads(x @ Wq.T + bq, B, S)
            k = _split_heads(x @ Wk.T + bk, B, S)
            v = _split_heads(x @ Wv.T + bv, B, S)
            q = jax.nn.relu(q)
            k = jax.nn.relu(k)
            k_sum = k.sum(axis=-1, keepdims=True)
            attn = jnp.einsum('bhnd,bhmd->bhnm', q, k) / (k_sum + EPS)
            attn = jax.nn.softmax(attn, axis=-1)
            out = jnp.einsum('bhnm,bhmd->bhnd', attn, v)
            out = out.transpose(0, 2, 1, 3).reshape(B, S, D_MODEL)
            return (out @ Wo.T + bo, attn)
        return _reference_tuple_inner(x, Wq, bq, Wk, bk, Wv, bv, Wo, bo)[0]

    def _L0_ffn_ref(hidden_states, gate_w, re_w1, re_b1, re_w2, re_b2, se_w1, se_b1, se_w2, se_b2):
        import jax, jax.numpy as jnp
        import numpy as np
        H = 128
        F = 512
        E = 16
        SHARED = 2
        TOP_K = 4
        B, S = (2, 512)

        def _mlp(x, w1, b1, w2, b2):
            return jax.nn.gelu(x @ w1 + b1, approximate=False) @ w2 + b2
        b, s, h = hidden_states.shape
        x = hidden_states.reshape(-1, h)
        gate_probs = jax.nn.softmax(x @ gate_w.T, axis=-1)
        top_v, top_i = jax.lax.top_k(gate_probs, TOP_K)
        top_v = jax.nn.softmax(top_v, axis=-1)
        combine = jnp.einsum('tk,tke->te', top_v, jax.nn.one_hot(top_i, E, dtype=x.dtype))
        routed = jnp.zeros_like(x)
        for e in range(E):
            routed = routed + combine[:, e:e + 1] * _mlp(x, re_w1[e], re_b1[e], re_w2[e], re_b2[e])
        shared = jnp.zeros_like(x)
        for j in range(SHARED):
            shared = shared + _mlp(x, se_w1[j], se_b1[j], se_w2[j], se_b2[j])
        shared = shared / SHARED
        return (routed + shared).reshape(b, s, h)
    h = _L0_tok_ref(x, L0_tok_W, L0_tok_b, L0_tok_gamma, L0_tok_beta)
    h = h + _L0_attn_ref(_layernorm(h, axis=-1), L0_attn_Wq, L0_attn_bq, L0_attn_Wk, L0_attn_bk, L0_attn_Wv, L0_attn_bv, L0_attn_Wo, L0_attn_bo)
    h = h + _L0_ffn_ref(_layernorm(h, axis=-1), L0_ffn_gate_w, L0_ffn_re_w1, L0_ffn_re_b1, L0_ffn_re_w2, L0_ffn_re_b2, L0_ffn_se_w1, L0_ffn_se_b1, L0_ffn_se_w2, L0_ffn_se_b2)
    return h

_drawn_inputs = setup_inputs


def setup_inputs(seed=0):
    import zlib

    import numpy as np

    out = dict(_drawn_inputs(seed))
    spreads = {'L0_tok_b': (0.0, 0.1),
     'L0_tok_gamma': (1.0, 0.2),
     'L0_tok_beta': (0.0, 0.1),
     'L0_ffn_re_b1': (0.0, 0.71),
     'L0_ffn_re_b2': (0.0, 0.1),
     'L0_ffn_se_b1': (0.0, 0.483),
     'L0_ffn_se_b2': (0.0, 0.1)}
    factors = {'L0_attn_Wq': 8.0,
     'L0_attn_bq': 8.0,
     'L0_attn_Wk': 8.0,
     'L0_attn_bk': 8.0,
     'L0_attn_Wv': 7.353,
     'L0_attn_bv': 8.0,
     'L0_attn_Wo': 7.129,
     'L0_attn_bo': 2.713}
    for name, (base, spread) in spreads.items():
        noise = np.random.default_rng([zlib.crc32(name.encode()), seed]).standard_normal(out[name].shape)
        drawn = base * np.exp(spread * noise) if base else spread * noise
        out[name] = jnp.asarray(drawn.astype(out[name].dtype))
    for name, factor in factors.items():
        out[name] = (out[name] * factor).astype(out[name].dtype)
    return out
```

```python
from contextlib import ExitStack

import concourse.bass as bass
from concourse import mybir

P = 128
F32 = mybir.dt.float32
ALU = mybir.AluOpType
ACT = mybir.ActivationFunctionType
AX = mybir.AxisListType

COLUMNS = [("tok_b", 1), ("tok_gamma", 1), ("tok_beta", 1), ("bk", 2), ("b1", 72)]
WIDE = [("wk", 256), ("wqv", 256), ("wo", 128), ("gate", 16), ("ident", 128), ("head_of", 16), ("rank", 16)]
ROWS = [("bqv", 256), ("bo", 128), ("ones", 128)]


def spans(groups):
    at, out = 0, {}
    for name, width in groups:
        out[name] = (at, at + width)
        at += width
    return out, at


def count(n, most):
    if isinstance(n, int):
        return None if n <= 0 else min(n, most)
    return n


def build(nc, xT, tok_w, columns, wide, rows, re_w1, re_w2, se_w1, se_w2, re_b2, se_b2, out):
    D, B, T = xT.shape
    CTX = tok_w.shape[0] // D
    S = T - CTX + 1
    C = tok_w.shape[1]
    H, DH = 8, 16
    HP = 2 * DH
    G = H * HP // P
    E, _, F = re_w1.shape
    SH = se_w1.shape[0]
    EX = E + SH
    FB = F // P
    K = 4
    CB = 4
    NCH = B // CB
    CW = CB * S
    BN_EPS = LN_EPS = 1e-5
    ATT_EPS = 1e-6
    col_at, col_n = spans(COLUMNS)
    wide_at, wide_n = spans(WIDE)
    row_at, row_n = spans(ROWS)

    with ExitStack() as ctx:
        def sb(name, shape):
            return ctx.enter_context(nc.sbuf_tensor(name, shape, F32))

        def sem(name):
            return ctx.enter_context(nc.semaphore(name))

        cols_sb = sb("cols_sb", [P, col_n])
        wide_sb = sb("wide_sb", [P, wide_n])
        rows_sb = sb("rows_sb", [1, row_n])
        tokw_sb = sb("tokw_sb", [CTX * D, C])
        w1_sb = sb("w1_sb", [P, EX, F])
        w2_sb = sb("w2_sb", [P, EX, FB, C])
        b2_sb = sb("b2_sb", [EX, C])
        xt_all = sb("xt_all", [P, B, S])
        hid_t = sb("hid_t", [P, B, S])
        y_all = sb("y_all", [S, B, C])
        bn_st = sb("bn_st", [P, NCH, 6])
        bn_mv = sb("bn_mv", [P, 2])
        bn_t = sb("bn_t", [P, 4])
        yt = sb("yt", [P, 2, S])
        ln_st = sb("ln_st", [S, 2, 6])
        st_all = sb("st_all", [S, B, 6])
        mean1 = sb("mean1", [S, B])
        mean2 = sb("mean2", [S, B])
        half_gap = sb("half_gap", [S, B])
        std1 = sb("std1", [S, B])
        rstd1 = sb("rstd1", [S, B])
        std2 = sb("std2", [S, B])
        rstd2 = sb("rstd2", [S, B])
        h2 = sb("h2", [S, 2, C])
        xln = sb("xln", [S, 2, C])
        xlnt = sb("xlnt", [P, 2, S])
        k_t = sb("k_t", [P, 4, G, S])
        q_sb = sb("q_sb", [S, 2, H, DH])
        kden = sb("kden", [S, 2, H])
        krec = sb("krec", [S, 2, H])
        qpad = sb("qpad", [S, 2, H, HP])
        q_t = sb("q_t", [P, 2, G, S])
        v_aug = sb("v_aug", [S, 4, H, DH + 1])
        smax = sb("smax", [S, 2, 2, 4])
        prob = sb("prob", [S, 2, 2, 4, S])
        prob_t = sb("prob_t", [S, 2, 2, 4, S])
        orec = sb("orec", [S, 2, H])
        onorm = sb("onorm", [S, 2, H, DH])
        o_t = sb("o_t", [P, 2, S])
        x2 = sb("x2", [S, 2, C])
        x2t = sb("x2t", [P, 2, S])
        logits = sb("logits", [S, B, E])
        left = sb("left", [S, B, E])
        hit = sb("hit", [S, B, E])
        pick = sb("pick", [S, K, B, E])
        top = sb("top", [S, K, B])
        first = sb("first", [S, B])
        zsum = sb("zsum", [S, B])
        zrec = sb("zrec", [S, B])
        gate_v = sb("gate_v", [S, K, B])
        comb = sb("comb", [S, B, EX])
        comb_b = sb("comb_b", [S, 2, EX])
        comb_t = sb("comb_t", [EX, 2, S])
        act_t = sb("act_t", [P, 2, FB, CW])

        ident = wide_sb[:, wide_at["ident"][0]:wide_at["ident"][1]]
        ident_s = ident[0:S, 0:S]
        wk = wide_sb[:, wide_at["wk"][0]:wide_at["wk"][1]].rearrange("p (g c) -> p g c", g=G)
        wqv = wide_sb[:, wide_at["wqv"][0]:wide_at["wqv"][1]]
        wo = wide_sb[:, wide_at["wo"][0]:wide_at["wo"][1]]
        gate_w = wide_sb[:, wide_at["gate"][0]:wide_at["gate"][1]]
        head_of = wide_sb[:, wide_at["head_of"][0]:wide_at["head_of"][1]].rearrange("p (g h) -> p g h", g=G)
        rank = wide_sb[0:S, wide_at["rank"][0]:wide_at["rank"][1]]
        bqv = rows_sb[0:1, row_at["bqv"][0]:row_at["bqv"][1]]
        bo = rows_sb[0:1, row_at["bo"][0]:row_at["bo"][1]]
        ones = rows_sb[0:1, row_at["ones"][0]:row_at["ones"][0] + S]

        def column(name, n=0):
            at = col_at[name][0] + n
            return cols_sb[:, at:at + 1]

        ps = ctx.enter_context(nc.psum_tensor("ps", [P, 8, 512], F32))
        M0, M1 = 6, 7

        frames_in = sem("frames_in")
        tokw_in = sem("tokw_in")
        params_in = sem("params_in")
        w_in = sem("w_in")
        stored = sem("stored")
        pads_zero = sem("pads_zero")
        tok_psum = sem("tok_psum")
        tok_sb = sem("tok_sb")
        tok_stats = sem("tok_stats")
        bn_step = sem("bn_step")
        bn_var = sem("bn_var")
        bn_std = sem("bn_std")
        yt_sb = sem("yt_sb")
        y_psum = sem("y_psum")
        y_sb = sem("y_sb")
        st_step = sem("st_step")
        y_stats = sem("y_stats")
        var1 = sem("var1")
        std1_ok = sem("std1_ok")
        rstd1_ok = sem("rstd1_ok")
        ln_step = sem("ln_step")
        ln_sum = sem("ln_sum")
        h2_kept = sem("h2_kept")
        x_ln = sem("x_ln")
        x_t_psum = sem("x_t_psum")
        x_t_sb = sem("x_t_sb")
        k_psum = sem("k_psum")
        k_sb = sem("k_sb")
        qv_psum = sem("qv_psum")
        qv_sb = sem("qv_sb")
        ks_psum = sem("ks_psum")
        ks_read = sem("ks_read")
        ks_rec = sem("ks_rec")
        q_scaled = sem("q_scaled")
        q_t_psum = sem("q_t_psum")
        q_t_sb = sem("q_t_sb")
        s_psum = sem("s_psum")
        s_max = sem("s_max")
        s_sub = sem("s_sub")
        s_exp = sem("s_exp")
        p_t_psum = sem("p_t_psum")
        p_t_sb = sem("p_t_sb")
        o_psum = sem("o_psum")
        o_rec = sem("o_rec")
        o_sb = sem("o_sb")
        o_t_psum = sem("o_t_psum")
        o_t_sb = sem("o_t_sb")
        pr_psum = sem("pr_psum")
        h2_sb = sem("h2_sb")
        h2_st = sem("h2_st")
        h2_mv = sem("h2_mv")
        var2 = sem("var2")
        std2_ok = sem("std2_ok")
        rstd2_ok = sem("rstd2_ok")
        x2_sb = sem("x2_sb")
        x2t_psum = sem("x2t_psum")
        x2t_sb = sem("x2t_sb")
        x2t_kept = sem("x2t_kept")
        lg_psum = sem("lg_psum")
        lg_sb = sem("lg_sb")
        gstep = sem("gstep")
        g_diff = sem("g_diff")
        g_exp = sem("g_exp")
        cb_sb = sem("cb_sb")
        cbt_psum = sem("cbt_psum")
        cbt_sb = sem("cbt_sb")
        b2_psum = sem("b2_psum")
        b2_added = sem("b2_added")
        f1_psum = sem("f1_psum")
        f1_sb = sem("f1_sb")
        f2_psum = sem("f2_psum")
        f2_added = sem("f2_added")

        def after(eng, s, n, most=B, per=1):
            n = count(n, most)
            if n is not None:
                eng.wait_ge(s, n * per if per != 1 else n)

        def slots(eng, slot):
            lo = 4
            hi = B - 4
            for i in range(-4, lo):
                slot(i, i % 4)
            with eng.Fori(lo, hi - 3, 4) as i:
                for u in range(4):
                    slot(i + u, (lo + u) % 4)
            for i in range(hi, B + 1):
                slot(i, i % 4)

        def lives(b):
            return not isinstance(b, int) or 0 <= b < B

        def pairs(eng, step, lag, lo):
            for i in range(lo):
                step(i, i % 2)
            with eng.Fori(lo, B - 1, 2) as i:
                for u in range(2):
                    step(i + u, u)
            for i in range(B, B + lag):
                step(i, i % 2)

        block = ctx.enter_context(nc.Block())

        @block.sync
        def _(sp):
            for i in range(CTX):
                sp.dma_start(xt_all[i * D:(i + 1) * D, :, :], xT[:, :, i:i + S]).then_inc(frames_in, 16)
            sp.dma_start(wide_sb[:, :], wide).then_inc(params_in, 16)
            sp.dma_start(rows_sb[:, :], rows).then_inc(params_in, 16)
            for e in range(0, E, 4):
                sp.dma_start(w1_sb[:, e:e + 4, :], re_w1[e:e + 4].rearrange("e h f -> h e f")).then_inc(w_in, 16)
                sp.dma_start(w2_sb[:, e:e + 4, :, :].rearrange("p e c h -> p (e c) h"),
                             re_w2[e:e + 4].rearrange("e (c p) h -> p (e c) h", p=P)).then_inc(w_in, 16)
            sp.dma_start(w1_sb[:, E:EX, :], se_w1.rearrange("e h f -> h e f")).then_inc(w_in, 16)
            sp.dma_start(w2_sb[:, E:EX, :, :].rearrange("p e c h -> p (e c) h"),
                         se_w2.rearrange("e (c p) h -> p (e c) h", p=P)).then_inc(w_in, 16)
            sp.dma_start(b2_sb[0:E, :], re_b2).then_inc(w_in, 16)
            sp.dma_start(b2_sb[E:EX, :], se_b2).then_inc(w_in, 16)
            with sp.Fori(0, NCH) as c:
                sp.wait_ge(f2_added, c * (EX * CB) + EX * CB)
                sp.dma_start(out.rearrange("b t c -> t b c")[:, bass.ts(c, CB), :],
                             y_all[:, bass.ts(c, CB), :]).then_inc(stored, 16)
            sp.wait_ge(stored, 16 * NCH)

        W_ALL = 16 * (2 * E // 4 + 4)

        @block.gpsimd
        def _(pool):
            nc.gpsimd.memset(qpad[:, :, :, :], 0.0).then_inc(pads_zero, 1)
            nc.gpsimd.memset(v_aug[:, :, :, :], 1.0).then_inc(pads_zero, 1)
            nc.gpsimd.memset(comb[:, :, :], 1.0 / SH).then_inc(pads_zero, 1)

            def keep_h2(b, p):
                pool.wait_ge(h2_sb, b + 1)
                nc.gpsimd.tensor_copy(y_all[:, b, :], h2[:, p, :]).then_inc(h2_kept, 1)

            pairs(pool, keep_h2, 0, 0)

            def step(b, p):
                pool.wait_ge(x2t_sb, b + 1)
                nc.gpsimd.tensor_copy(xt_all[:, b, :], x2t[:, p, :]).then_inc(x2t_kept, 1)

            pairs(pool, step, 0, 0)

        @block.tensor
        def _(pe):
            pe.wait_ge(frames_in, 16 * CTX)
            pe.wait_ge(tokw_in, 32)

            def tok_chunk(c, p):
                after(pe, tok_sb, c - 1, NCH)
                nc.tensor.matmul(ps[:, p, 0:CW], tokw_sb[:, :], xt_all[0:CTX * D, bass.ts(c, CB), :],
                                 start=True, stop=True).then_inc(tok_psum, 1)

            tok_chunk(0, 0)
            tok_chunk(1, 1)
            with pe.Fori(2, NCH - 1, 2) as c:
                tok_chunk(c, 0)
                tok_chunk(c + 1, 1)

            pe.wait_ge(params_in, 32)

            def turn_y(b, p):
                pe.wait_ge(yt_sb, b + 1)
                after(pe, st_step, b - 1)
                nc.tensor.transpose(ps[0:S, 2 + p, 0:C], yt[:, p, :], ident).then_inc(y_psum, 1)

            pairs(pe, turn_y, 0, 2)

            def slot(i, r):
                steady = not isinstance(i, int)

                def m0_free(x, o, k, q):
                    for s, n, per in ((x_t_sb, x, 1), (o_t_sb, o, 1), (k_sb, k, G), (q_t_sb, q, 1)):
                        if n is not None:
                            after(pe, s, n, per=per)

                def m1_free(ks, pr, qv, o):
                    for s, n, per in ((ks_read, ks, 1), (h2_sb, pr, 1), (qv_sb, qv, 2), (o_sb, o, 1)):
                        if n is not None:
                            after(pe, s, n, per=per)

                def scores(half):
                    b = i + 1
                    if not lives(b):
                        return
                    if half == 0:
                        pe.wait_ge(q_t_sb, b + 1)
                    after(pe, s_sub, 2 * b - 1 + half, 2 * B)
                    for j in (2 * half, 2 * half + 1):
                        for g in range(G):
                            rows_j = slice(HP * j, HP * j + HP)
                            mm = nc.tensor.matmul(ps[0:S, j, g * S:(g + 1) * S], q_t[rows_j, (r + 1) % 2, g, :],
                                                  k_t[rows_j, (r + 1) % 4, g, :], start=True, stop=True)
                    mm.then_inc(s_psum, 1)

                def turn_prob(half):
                    b = i
                    if not lives(b):
                        return
                    pe.wait_ge(s_exp, 2 * b + half + 1)
                    after(pe, p_t_sb, 2 * b - 1 + half, 2 * B)
                    for n in range(4):
                        mm = nc.tensor.transpose(ps[0:S, 4 + half, n * S:(n + 1) * S],
                                                 prob[:, r % 2, half, n, :], ident_s)
                    mm.then_inc(p_t_psum, 1)

                scores(0)
                if lives(i + 3):
                    b = i + 3
                    pe.wait_ge(x_ln, b + 1)
                    m0_free(*((None, None, None, b - 1) if steady else (b, b - 4, b, b - 1)))
                    nc.tensor.transpose(ps[:, M0, 0:S], xln[:, (r + 3) % 2, :], ident_s).then_inc(x_t_psum, 1)
                if lives(i + 2):
                    b = i + 2
                    after(pe, k_sb, b + 1, per=G)
                    m1_free(*((None, None, None, b - 2) if steady else (b, b - 3, b + 1, b - 2)))
                    for g in range(G):
                        mm = nc.tensor.matmul(ps[0:S, M1, 256:256 + H], k_t[:, (r + 2) % 4, g, :], head_of[:, g, :],
                                              start=(g == 0), stop=(g == G - 1))
                    mm.then_inc(ks_psum, 1)
                scores(1)
                if lives(i - 1):
                    b = i - 1
                    pe.wait_ge(o_sb, b + 1)
                    m0_free(*((b + 5, None, None, None) if steady else (b + 5, b, b + 4, b + 3)))
                    nc.tensor.transpose(ps[:, M0, 0:S], onorm[:, (r + 3) % 2, :, :].rearrange("s h d -> s (h d)"),
                                        ident_s).then_inc(o_t_psum, 1)
                turn_prob(0)
                if lives(i + 3):
                    b = i + 3
                    pe.wait_ge(x_t_sb, b + 1)
                    m0_free(*((None, b - 3, None, None) if steady else (b + 1, b - 3, b, b - 1)))
                    for g in range(G):
                        mm = nc.tensor.matmul(ps[:, M0, g * S:(g + 1) * S], wk[:, g, :], xlnt[:, (r + 3) % 2, :],
                                              start=True, stop=True)
                    mm.then_inc(k_psum, 1)
                turn_prob(1)
                if lives(i - 1):
                    b = i - 1
                    pe.wait_ge(o_t_sb, b + 1)
                    m1_free(*((b + 4, None, None, None) if steady else (b + 4, b, b + 4, b + 1)))
                    nc.tensor.matmul(ps[0:S, M1, 0:C], ones, bo, start=True, stop=False)
                    nc.tensor.matmul(ps[0:S, M1, 0:C], o_t[:, (r + 3) % 2, :], wo,
                                     start=False, stop=True).then_inc(pr_psum, 1)
                if lives(i + 2):
                    b = i + 2
                    pe.wait_ge(q_scaled, b + 1)
                    m0_free(*((None, None, b + 2, None) if steady else (b + 2, b - 2, b + 2, b)))
                    for g in range(G):
                        mm = nc.tensor.transpose(ps[:, M0, g * S:(g + 1) * S],
                                                 qpad[:, r % 2, g * 4:(g + 1) * 4, :].rearrange("s h d -> s (h d)"),
                                                 ident_s)
                    mm.then_inc(q_t_psum, 1)
                if lives(i + 3):
                    b = i + 3
                    m1_free(*((None, b - 3, None, None) if steady else (b, b - 3, b, b - 3)))
                    nc.tensor.matmul(ps[0:S, M1, 0:2 * C], ones, bqv, start=True, stop=False)
                    nc.tensor.matmul(ps[0:S, M1, 0:2 * C], xlnt[:, (r + 3) % 2, :], wqv,
                                     start=False, stop=True).then_inc(qv_psum, 1)
                if lives(i):
                    b = i
                    pe.wait_ge(p_t_sb, 2 * b + 2)
                    m1_free(*((None, None, b + 4, None) if steady else (b + 3, b, b + 4, b)))
                    for half in range(2):
                        for n in range(4):
                            h = 4 * (n % 2) + 2 * half + n // 2
                            at = 264 + h * (DH + 1)
                            mm = nc.tensor.matmul(ps[0:S, M1, at:at + DH + 1], prob_t[:, r % 2, half, n, :],
                                                  v_aug[:, r % 4, h, :], start=True, stop=True)
                    mm.then_inc(o_psum, 1)

            slots(pe, slot)

            def gate_step(b, p):
                if lives(b):
                    pe.wait_ge(x2_sb, b + 1)
                    after(pe, x2t_sb, b - 1)
                    nc.tensor.transpose(ps[:, p, 0:S], x2[:, p, :], ident_s).then_inc(x2t_psum, 1)
                if lives(b - 1):
                    pe.wait_ge(x2t_sb, b)
                    after(pe, lg_sb, b - 2)
                    nc.tensor.matmul(ps[0:S, 3 - p, 0:E], x2t[:, 1 - p, :], gate_w,
                                     start=True, stop=True).then_inc(lg_psum, 1)

            pairs(pe, gate_step, 1, 4)

            pe.wait_ge(w_in, W_ALL)

            def bias_step(b, p):
                if lives(b):
                    pe.wait_ge(cb_sb, b + 1)
                    after(pe, cbt_sb, b - 1)
                    nc.tensor.transpose(ps[0:EX, 4 + p, 0:S], comb_b[:, p, :], ident_s).then_inc(cbt_psum, 1)
                if lives(b - 1):
                    pe.wait_ge(cbt_sb, b)
                    after(pe, b2_added, b - 2)
                    nc.tensor.matmul(ps[0:S, 7 - p, 0:C], comb_t[:, 1 - p, :], b2_sb[:, :],
                                     start=True, stop=True).then_inc(b2_psum, 1)

            pairs(pe, bias_step, 1, 4)

            pe.wait_ge(x2t_kept, B)
            pe.wait_ge(b2_added, B)

            def up(c, e, n):
                for fb in range(FB):
                    if fb == 0:
                        pass
                    v = count(n * FB + fb + 1 - FB, 10 ** 6)
                    if v is not None:
                        pe.wait_ge(f1_sb, v)
                    nc.tensor.matmul(ps[:, fb, 0:CW], w1_sb[:, e, fb * P:(fb + 1) * P],
                                     xt_all[:, bass.ts(c, CB), :], start=True, stop=True).then_inc(f1_psum, 1)

            def down(n, e):
                pe.wait_ge(f1_sb, n * FB + FB)
                v = count((n - 1) * CB, 10 ** 6)
                if v is not None:
                    pe.wait_ge(f2_added, v)
                for s in range(CB):
                    for fb in range(FB):
                        mm = nc.tensor.matmul(ps[0:S, 4 + e % 2, s * C:(s + 1) * C],
                                              act_t[:, e % 2, fb, s * S:(s + 1) * S], w2_sb[:, e, fb, :],
                                              start=(fb == 0), stop=(fb == FB - 1))
                    mm.then_inc(f2_psum, 1)

            def chunk(c):
                up(c, 0, c * EX)
                for e in range(EX):
                    if e + 1 < EX:
                        up(c, e + 1, c * EX + e + 1)
                    down(c * EX + e, e)

            chunk(0)
            with pe.Fori(1, NCH) as c:
                chunk(c)

        @block.scalar
        def _(act):
            act.dma_start(tokw_sb[:, :], tok_w).then_inc(tokw_in, 16)
            act.dma_start(cols_sb[:, :], columns).then_inc(tokw_in, 16)
            act.wait_ge(tokw_in, 32)
            with act.Fori(0, NCH - 1, 2) as c0:
                for u in range(2):
                    c = c0 + u
                    act.wait_ge(tok_psum, c + 1)
                    nc.scalar.activation(hid_t[:, bass.ts(c, CB), :].rearrange("p b s -> p (b s)"), ps[:, u, 0:CW],
                                         ACT.Relu, bias=column("tok_b")).then_inc(tok_sb, 1)
            act.wait_ge(bn_var, 1)
            nc.scalar.activation(bn_t[:, 1:2], bn_t[:, 0:1], ACT.Sqrt).then_inc(bn_std, 1)

            def keep_y(b, p):
                act.wait_ge(y_psum, b + 1)
                nc.scalar.copy(y_all[:, b, :], ps[0:S, 2 + p, 0:C]).then_inc(y_sb, 1)

            pairs(act, keep_y, 0, 0)
            act.wait_ge(var1, 1)
            nc.scalar.activation(std1[:, :], rstd1[:, :], ACT.Sqrt).then_inc(std1_ok, 1)
            act.wait_ge(params_in, 32)

            def slot(i, r):
                def exp(half):
                    b = i + 1
                    if lives(b):
                        act.wait_ge(s_sub, 2 * b + half + 1)
                        x = prob[:, (r + 1) % 2, half, :, :]
                        nc.scalar.activation(x, x, ACT.Exp).then_inc(s_exp, 1)

                def keep_prob_t(half):
                    b = i
                    if lives(b):
                        act.wait_ge(p_t_psum, 2 * b + half + 1)
                        after(act, o_psum, b - 1)
                        nc.scalar.copy(prob_t[:, r % 2, half, :, :].rearrange("s n t -> s (n t)"),
                                       ps[0:S, 4 + half, 0:4 * S]).then_inc(p_t_sb, 1)

                if lives(i + 3):
                    b = i + 3
                    act.wait_ge(x_t_psum, b + 1)
                    after(act, qv_psum, b - 1)
                    nc.scalar.copy(xlnt[:, (r + 3) % 2, :], ps[:, M0, 0:S]).then_inc(x_t_sb, 1)
                if lives(i - 1):
                    b = i - 1
                    act.wait_ge(o_t_psum, b + 1)
                    after(act, pr_psum, b - 1)
                    nc.scalar.copy(o_t[:, (r + 3) % 2, :], ps[:, M0, 0:S]).then_inc(o_t_sb, 1)
                exp(0)
                keep_prob_t(0)
                if lives(i + 3):
                    b = i + 3
                    act.wait_ge(k_psum, b + 1)
                    after(act, s_psum, 2 * b - 6, 2 * B)
                    for g in range(G):
                        nc.scalar.activation(k_t[:, (r + 3) % 4, g, :], ps[:, M0, g * S:(g + 1) * S], ACT.Relu,
                                             bias=column("bk", g)).then_inc(k_sb, 1)
                exp(1)
                keep_prob_t(1)
                if lives(i + 2):
                    b = i + 2
                    act.wait_ge(q_t_psum, b + 1)
                    after(act, s_psum, 2 * b - 2, 2 * B)
                    nc.scalar.copy(q_t[:, r % 2, :, :].rearrange("p g s -> p (g s)"),
                                   ps[:, M0, 0:G * S]).then_inc(q_t_sb, 1)

            slots(act, slot)
            act.wait_ge(var2, 1)
            nc.scalar.activation(std2[:, :], rstd2[:, :], ACT.Sqrt).then_inc(std2_ok, 1)

            def keep_x2t(b, p):
                act.wait_ge(x2t_psum, b + 1)
                after(act, lg_psum, b - 1)
                after(act, x2t_kept, b - 1)
                nc.scalar.copy(x2t[:, p, :], ps[:, p, 0:S]).then_inc(x2t_sb, 1)

            pairs(act, keep_x2t, 0, 2)

            act.wait_ge(g_diff, 2)
            nc.scalar.activation(left[:, :, :], left[:, :, :], ACT.Exp).then_inc(g_exp, 1)
            nc.scalar.activation(gate_v[:, :, :], gate_v[:, :, :], ACT.Exp).then_inc(g_exp, 1)
            act.wait_ge(g_diff, 3)
            nc.scalar.activation(gate_v[:, :, :], gate_v[:, :, :], ACT.Exp).then_inc(g_exp, 1)

            def keep_comb_t(b, p):
                act.wait_ge(cbt_psum, b + 1)
                after(act, b2_psum, b - 1)
                nc.scalar.copy(comb_t[:, p, :], ps[0:EX, 4 + p, 0:S]).then_inc(cbt_sb, 1)

            pairs(act, keep_comb_t, 0, 2)

            def chunk(c):
                for e in range(EX):
                    n = c * EX + e
                    v = count((n - 1) * CB, 10 ** 6)
                    if v is not None:
                        act.wait_ge(f2_psum, v)
                    for fb in range(FB):
                        act.wait_ge(f1_psum, n * FB + fb + 1)
                        nc.scalar.activation(act_t[:, e % 2, fb, :], ps[:, fb, 0:CW], ACT.Gelu,
                                             bias=column("b1", e * FB + fb)).then_inc(f1_sb, 1)

            chunk(0)
            with act.Fori(1, NCH) as c:
                chunk(c)

        @block.vector
        def _(dve):
            v = nc.vector
            dve.wait_ge(tokw_in, 32)
            for c in range(NCH):
                dve.wait_ge(tok_sb, c + 1)
                v.bn_stats(bn_st[:, c, :], hid_t[:, c * CB:(c + 1) * CB, :].rearrange("p b s -> p (b s)"))\
                 .then_inc(tok_stats, 1)
            dve.wait_ge(tok_stats, NCH)
            v.bn_aggr(bn_mv[:, :], bn_st[:, :, :]).then_inc(bn_step, 1)
            dve.wait_ge(bn_step, 1)
            v.tensor_scalar(bn_t[:, 0:1], bn_mv[:, 1:2], BN_EPS, None, ALU.add).then_inc(bn_var, 1)
            dve.wait_ge(bn_std, 1)
            v.reciprocal(bn_t[:, 2:3], bn_t[:, 1:2]).then_inc(bn_step, 1)
            dve.wait_ge(bn_step, 2)
            v.tensor_tensor(bn_t[:, 2:3], bn_t[:, 2:3], column("tok_gamma"), ALU.mult).then_inc(bn_step, 1)
            dve.wait_ge(bn_step, 3)
            v.scalar_tensor_tensor(bn_t[:, 3:4], bn_mv[:, 0:1], bn_t[:, 2:3], column("tok_beta"),
                                   ALU.mult, ALU.subtract).then_inc(bn_step, 1)
            dve.wait_ge(bn_step, 4)

            def join_stats(mean, var, done, ready):
                v.tensor_tensor(mean[:, :], st_all[:, :, 1], st_all[:, :, 4], ALU.add).then_inc(ln_step, 1)
                v.tensor_tensor(half_gap[:, :], st_all[:, :, 1], st_all[:, :, 4], ALU.subtract).then_inc(ln_step, 1)
                dve.wait_ge(ln_step, done + 2)
                v.tensor_scalar(mean[:, :], mean[:, :], 0.5, None, ALU.mult).then_inc(ln_step, 1)
                v.scalar_tensor_tensor(half_gap[:, :], half_gap[:, :], 0.25 * C, half_gap[:, :],
                                       ALU.mult, ALU.mult).then_inc(ln_step, 1)
                dve.wait_ge(ln_step, done + 4)
                v.tensor_tensor(var[:, :], st_all[:, :, 2], st_all[:, :, 5], ALU.add).then_inc(ln_sum, 1)
                dve.wait_ge(ln_sum, done // 2 + 1)
                v.tensor_tensor(var[:, :], var[:, :], half_gap[:, :], ALU.add).then_inc(ln_sum, 1)
                dve.wait_ge(ln_sum, done // 2 + 2)
                v.tensor_scalar(var[:, :], var[:, :], 1.0 / C, LN_EPS, ALU.mult, ALU.add).then_inc(ready, 1)

            def y_step(b, p):
                if lives(b):
                    after(dve, y_psum, b - 1)
                    v.tensor_scalar(yt[:, p, :], hid_t[:, b, :], bn_t[:, 2:3], bn_t[:, 3:4],
                                    ALU.mult, ALU.subtract).then_inc(yt_sb, 1)
                if lives(b - 2):
                    d = b - 2
                    dve.wait_ge(y_sb, d + 1)
                    after(dve, y_stats, d - 1)
                    v.bn_stats(ln_st[:, p, :], ps[0:S, 2 + p, 0:C]).then_inc(st_step, 1)
                    dve.wait_ge(st_step, d + 1)
                    v.tensor_copy(st_all[:, d, :], ln_st[:, p, :]).then_inc(y_stats, 1)

            pairs(dve, y_step, 2, 4)
            dve.wait_ge(y_stats, B)
            join_stats(mean1, rstd1, 0, var1)
            dve.wait_ge(std1_ok, 1)
            v.reciprocal(rstd1[:, :], std1[:, :]).then_inc(rstd1_ok, 1)
            dve.wait_ge(rstd1_ok, 1)
            dve.wait_ge(pads_zero, 3)

            def slot(i, r):
                def row_max(half):
                    b = i + 1
                    if not lives(b):
                        return
                    dve.wait_ge(s_psum, 2 * b + half + 1)
                    after(dve, p_t_psum, 2 * b - 3 + half, 2 * B)
                    scores = ps[0:S, 2 * half:2 * half + 2, 0:G * S].rearrange("s j (g t) -> s j g t", g=G)
                    top4 = smax[:, (r + 1) % 2, half, :].rearrange("s (j g) -> s j g", g=G)
                    v.tensor_reduce(top4, scores, AX.X, ALU.max).then_inc(s_max, 1)
                    dve.wait_ge(s_max, 2 * b + half + 1)
                    v.tensor_tensor(prob[:, (r + 1) % 2, half, :, :].rearrange("s (j g) t -> s j g t", g=G), scores,
                                    top4.unsqueeze(3).broadcast_to([S, 2, G, S]), ALU.subtract).then_inc(s_sub, 1)

                if lives(i + 2):
                    b = i + 2
                    dve.wait_ge(ks_psum, b + 1)
                    v.tensor_scalar(kden[:, r % 2, :], ps[0:S, M1, 256:256 + H], ATT_EPS, None,
                                    ALU.add).then_inc(ks_read, 1)
                    dve.wait_ge(ks_read, b + 1)
                    v.reciprocal(krec[:, r % 2, :], kden[:, r % 2, :]).then_inc(ks_rec, 1)
                    dve.wait_ge(ks_rec, b + 1)
                    dve.wait_ge(qv_sb, 2 * b + 2)
                    after(dve, q_t_psum, b - 1)
                    v.tensor_tensor(qpad[:, r % 2, :, 0:DH], q_sb[:, r % 2, :, :],
                                    krec[:, r % 2, :].unsqueeze(2).broadcast_to([S, H, DH]),
                                    ALU.mult).then_inc(q_scaled, 1)
                row_max(0)
                row_max(1)
                if lives(i - 1):
                    b = i - 1
                    dve.wait_ge(pr_psum, b + 1)
                    after(dve, h2_kept, b - 1)
                    v.tensor_tensor(h2[:, (r + 3) % 2, :], ps[0:S, M1, 0:C], y_all[:, b, :],
                                    ALU.add).then_inc(h2_sb, 1)
                    dve.wait_ge(h2_sb, b + 1)
                    v.bn_stats(ln_st[:, (r + 3) % 2, :], h2[:, (r + 3) % 2, :]).then_inc(h2_st, 1)
                    dve.wait_ge(h2_st, b + 1)
                    v.tensor_copy(st_all[:, b, :], ln_st[:, (r + 3) % 2, :]).then_inc(h2_mv, 1)
                if lives(i + 4):
                    b = i + 4
                    after(dve, x_t_psum, b - 1)
                    v.tensor_scalar(xln[:, r % 2, :], y_all[:, b, :], mean1[:, bass.ds(b, 1)],
                                    rstd1[:, bass.ds(b, 1)], ALU.subtract, ALU.mult).then_inc(x_ln, 1)
                if lives(i + 3):
                    b = i + 3
                    dve.wait_ge(qv_psum, b + 1)
                    after(dve, q_scaled, b - 1)
                    v.tensor_scalar(q_sb[:, (r + 3) % 2, :, :].rearrange("s h d -> s (h d)"), ps[0:S, M1, 0:C], 0.0,
                                    None, ALU.max).then_inc(qv_sb, 1)
                    after(dve, o_psum, b - 3)
                    v.tensor_copy(v_aug[:, (r + 3) % 4, :, 0:DH],
                                  ps[0:S, M1, C:2 * C].rearrange("s (h d) -> s h d", d=DH)).then_inc(qv_sb, 1)
                if lives(i):
                    b = i
                    dve.wait_ge(o_psum, b + 1)
                    o = ps[0:S, M1, 264:264 + H * (DH + 1)].rearrange("s (h d) -> s h d", d=DH + 1)
                    v.reciprocal(orec[:, r % 2, :], o[:, :, DH]).then_inc(o_rec, 1)
                    dve.wait_ge(o_rec, b + 1)
                    after(dve, o_t_psum, b - 1)
                    v.tensor_tensor(onorm[:, r % 2, :, :], o[:, :, 0:DH],
                                    orec[:, r % 2, :].unsqueeze(2).broadcast_to([S, H, DH]),
                                    ALU.mult).then_inc(o_sb, 1)

            slots(dve, slot)
            dve.wait_ge(h2_mv, B)
            dve.wait_ge(h2_kept, B)
            join_stats(mean2, rstd2, 4, var2)
            dve.wait_ge(std2_ok, 1)
            v.reciprocal(rstd2[:, :], std2[:, :]).then_inc(rstd2_ok, 1)
            dve.wait_ge(rstd2_ok, 1)

            def gate_step(b, p):
                if lives(b):
                    after(dve, x2t_psum, b - 1)
                    v.tensor_scalar(x2[:, p, :], y_all[:, b, :], mean2[:, bass.ds(b, 1)], rstd2[:, bass.ds(b, 1)],
                                    ALU.subtract, ALU.mult).then_inc(x2_sb, 1)
                if lives(b - 2):
                    dve.wait_ge(lg_psum, b - 1)
                    v.tensor_copy(logits[:, b - 2, :], ps[0:S, 2 + p, 0:E]).then_inc(lg_sb, 1)

            pairs(dve, gate_step, 2, 4)
            dve.wait_ge(lg_sb, B)

            steps = [0]

            def then(ins):
                steps[0] += 1
                ins.then_inc(gstep, 1)
                dve.wait_ge(gstep, steps[0])

            wide3 = [S, B, E]
            then(v.tensor_copy(left[:, :, :], logits[:, :, :]))
            for k in range(K):
                then(v.tensor_reduce(top[:, k, :], left[:, :, :], AX.X, ALU.max))
                then(v.tensor_tensor(hit[:, :, :], left[:, :, :], top[:, k, :].unsqueeze(2).broadcast_to(wide3),
                                     ALU.is_ge))
                then(v.tensor_tensor(hit[:, :, :], hit[:, :, :], rank.unsqueeze(1).broadcast_to(wide3), ALU.mult))
                then(v.tensor_reduce(first[:, :], hit[:, :, :], AX.X, ALU.max))
                then(v.tensor_tensor(pick[:, k, :, :], hit[:, :, :], first[:, :].unsqueeze(2).broadcast_to(wide3),
                                     ALU.is_equal))
                then(v.scalar_tensor_tensor(left[:, :, :], pick[:, k, :, :], -3.0e38, left[:, :, :],
                                            ALU.mult, ALU.add))
            v.tensor_tensor(left[:, :, :], logits[:, :, :], top[:, 0, :].unsqueeze(2).broadcast_to(wide3),
                            ALU.subtract).then_inc(g_diff, 1)
            v.tensor_tensor(gate_v[:, :, :], top[:, :, :], top[:, 0, :].unsqueeze(1).broadcast_to([S, K, B]),
                            ALU.subtract).then_inc(g_diff, 1)
            dve.wait_ge(g_exp, 2)
            then(v.tensor_reduce(zsum[:, :], left[:, :, :], AX.X, ALU.add))
            then(v.reciprocal(zrec[:, :], zsum[:, :]))
            then(v.tensor_tensor(gate_v[:, :, :], gate_v[:, :, :], zrec[:, :].unsqueeze(1).broadcast_to([S, K, B]),
                                 ALU.mult))
            then(v.tensor_copy(first[:, :], gate_v[:, 0, :]))
            v.tensor_tensor(gate_v[:, :, :], gate_v[:, :, :], first[:, :].unsqueeze(1).broadcast_to([S, K, B]),
                            ALU.subtract).then_inc(g_diff, 1)
            dve.wait_ge(g_exp, 3)
            then(v.tensor_reduce(zsum[:, :], gate_v[:, :, :].rearrange("s k b -> s b k"), AX.X, ALU.add))
            then(v.reciprocal(zrec[:, :], zsum[:, :]))
            then(v.tensor_tensor(gate_v[:, :, :], gate_v[:, :, :], zrec[:, :].unsqueeze(1).broadcast_to([S, K, B]),
                                 ALU.mult))
            for k in range(K):
                dst = comb[:, :, 0:E] if k == 0 else hit[:, :, :]
                then(v.tensor_tensor(dst, pick[:, k, :, :], gate_v[:, k, :].unsqueeze(2).broadcast_to(wide3), ALU.mult))
                if k:
                    then(v.tensor_tensor(comb[:, :, 0:E], comb[:, :, 0:E], hit[:, :, :], ALU.add))

            def bias_step(b, p):
                if lives(b):
                    after(dve, cbt_psum, b - 1)
                    v.tensor_copy(comb_b[:, p, :], comb[:, b, :]).then_inc(cb_sb, 1)
                if lives(b - 2):
                    d = b - 2
                    dve.wait_ge(b2_psum, d + 1)
                    v.tensor_tensor(y_all[:, d, :], ps[0:S, 6 + p, 0:C], y_all[:, d, :], ALU.add).then_inc(b2_added, 1)

            pairs(dve, bias_step, 2, 4)
            dve.wait_ge(b2_added, B)

            def chunk(c):
                for e in range(EX):
                    n = c * EX + e
                    dve.wait_ge(f2_psum, n * CB + CB)
                    if e:
                        dve.wait_ge(f2_added, n * CB)
                    for s in range(CB):
                        b = c * CB + s
                        v.scalar_tensor_tensor(y_all[:, b, :], ps[0:S, 4 + e % 2, s * C:(s + 1) * C],
                                               comb[:, b, e:e + 1], y_all[:, b, :],
                                               ALU.mult, ALU.add).then_inc(f2_added, 1)

            chunk(0)
            with dve.Fori(1, NCH) as c:
                chunk(c)


def kernel(**inputs):
    import numpy as np
    import concourse.bacc as bacc
    from concourse import mybir as mb
    from concourse.bass_utils import run_bass_kernel_spmd

    a = {k: np.asarray(v) for k, v in inputs.items()}
    H, DH = 8, 16
    C = a["L0_tok_W"].shape[0]
    E, _, F = a["L0_ffn_re_w1"].shape
    B, T, D = a["x"].shape
    f32 = np.float32

    def padded_heads(w):
        o = np.zeros(w.shape[:-1] + (H, 2 * DH), f32)
        o[..., :DH] = w.reshape(w.shape[:-1] + (H, DH))
        return o.reshape(w.shape[:-1] + (2 * H * DH,))

    head_of = np.zeros((2, P, H), f32)
    for h in range(H):
        head_of[h // 4, 32 * (h % 4):32 * (h % 4) + DH, h] = 1.0
    b1 = np.concatenate([a["L0_ffn_re_b1"], a["L0_ffn_se_b1"]]).reshape(-1, P).T
    columns = np.concatenate([a["L0_tok_b"][:, None], a["L0_tok_gamma"][:, None], a["L0_tok_beta"][:, None],
                              padded_heads(a["L0_attn_bk"]).reshape(2, P).T, b1], axis=1)
    wide = np.concatenate([padded_heads(a["L0_attn_Wk"].T), a["L0_attn_Wq"].T, a["L0_attn_Wv"].T, a["L0_attn_Wo"].T,
                           a["L0_ffn_gate_w"].T, np.eye(P, dtype=f32),
                           head_of.transpose(1, 0, 2).reshape(P, 2 * H),
                           np.broadcast_to(np.arange(E, 0, -1, dtype=f32), (P, E))], axis=1)
    rows = np.concatenate([a["L0_attn_bq"], a["L0_attn_bv"], a["L0_attn_bo"], np.ones(P, f32)])[None, :]
    arrays = {"xT": a["x"].transpose(2, 0, 1), "tok_w": a["L0_tok_W"].T, "columns": columns, "wide": wide,
              "rows": rows, "re_w1": a["L0_ffn_re_w1"], "re_w2": a["L0_ffn_re_w2"], "se_w1": a["L0_ffn_se_w1"],
              "se_w2": a["L0_ffn_se_w2"], "re_b2": a["L0_ffn_re_b2"], "se_b2": a["L0_ffn_se_b2"]}
    arrays = {k: np.ascontiguousarray(v) for k, v in arrays.items()}

    nc = bacc.Bacc("TRN2", target_bir_lowering=False, num_devices=1)
    args = [nc.dram_tensor(k, v.shape, mb.dt.from_np(v.dtype), kind="ExternalInput").ap() for k, v in arrays.items()]
    S = T - a["L0_tok_W"].shape[1] // D + 1
    args.append(nc.dram_tensor("y", (B, S, C), mb.dt.float32, kind="ExternalOutput").ap())
    build(nc, *args)
    return run_bass_kernel_spmd(nc, [arrays], core_ids=[0]).results[0]["y"]
```

```python
from contextlib import ExitStack

import concourse.bass as bass
from concourse import mybir

P = 128
F32 = mybir.dt.float32
ALU = mybir.AluOpType
ACT = mybir.ActivationFunctionType
AX = mybir.AxisListType

COLUMNS = [("tok_b", 1), ("tok_gamma", 1), ("tok_beta", 1), ("bk", 2), ("b1", 8), ("bv", 1)]
WIDE = [("wk", 256), ("wqv", 256), ("wo", 128), ("gate", 16), ("ident", 128), ("head_of", 16), ("rank", 16),
        ("before", 128), ("every", 128), ("before_e", 256), ("bq", 128)]
ROWS = [("bo", 128), ("ones", 128), ("tile_no", 136)]


def spans(groups):
    at, out = 0, {}
    for name, width in groups:
        out[name] = (at, at + width)
        at += width
    return out, at


def count(n, most):
    if isinstance(n, int):
        return None if n <= 0 else min(n, most)
    return n


def build(nc, xT, tok_w, columns, wide, rows, re_w1, re_w2, se_w1, se_w2, re_b2, se_b2, re_b1, out):
    D, B, T = xT.shape
    CTX = tok_w.shape[0] // D
    S = T - CTX + 1
    C = tok_w.shape[1]
    H, DH = 8, 16
    HP = 2 * DH
    G = H * HP // P
    E, _, F = re_w1.shape
    SH = se_w1.shape[0]
    EX = E + SH
    FB = F // P
    K = 4
    CB = 4
    NCH = B // CB
    CW = CB * S
    N = B * S
    TS = P
    NT = (K * N + E * (TS - 1)) // TS
    WE = F + FB + FB * C
    MAGIC = 12582912.0
    BN_EPS = LN_EPS = 1e-5
    ATT_EPS = 1e-6
    col_at, col_n = spans(COLUMNS)
    wide_at, wide_n = spans(WIDE)
    row_at, row_n = spans(ROWS)

    with ExitStack() as ctx:
        def sb(name, shape):
            return ctx.enter_context(nc.sbuf_tensor(name, shape, F32))

        def sem(name):
            return ctx.enter_context(nc.semaphore(name))

        cols_sb = sb("cols_sb", [P, col_n])
        wide_sb = sb("wide_sb", [P, wide_n])
        rows_sb = sb("rows_sb", [1, row_n])
        tokw_sb = sb("tokw_sb", [CTX * D, C])
        w_all = sb("w_all", [P, E, WE])
        w1_sb = sb("w1_sb", [P, SH, F])
        w2_sb = sb("w2_sb", [P, SH, FB, C])
        b2_sb = sb("b2_sb", [EX, C])
        xt_all = sb("xt_all", [P, B, S])
        store = sb("store", [P, B * C])
        hid_t = store[:, 0:B * S].rearrange("p (b s) -> p b s", b=B)
        x2_all = store[0:S, :].rearrange("p (b c) -> p b c", b=B)
        y_all = sb("y_all", [S, B, C])
        bn_st = sb("bn_st", [P, NCH, 6])
        bn_mv = sb("bn_mv", [P, 2])
        bn_t = sb("bn_t", [P, 4])
        yt = sb("yt", [P, 2, S])
        ln_st = sb("ln_st", [S, 2, 6])
        st_all = sb("st_all", [S, B, 6])
        mean1 = sb("mean1", [S, B])
        mean2 = sb("mean2", [S, B])
        half_gap = sb("half_gap", [S, B])
        std1 = sb("std1", [S, B])
        rstd1 = sb("rstd1", [S, B])
        std2 = sb("std2", [S, B])
        rstd2 = sb("rstd2", [S, B])
        h2 = sb("h2", [S, 2, C])
        xln = sb("xln", [S, 2, C])
        xlnt = sb("xlnt", [P, 2, S])
        w_t = sb("w_t", [P, 4, WE])
        w_flat = w_t[:, :, :].rearrange("p n w -> p (n w)")
        prob = w_flat[0:S, 0:16 * S].rearrange("s (p h n t) -> s p h n t", p=2, h=2, n=4)
        prob_t = w_flat[0:S, 16 * S:32 * S].rearrange("s (p h n t) -> s p h n t", p=2, h=2, n=4)
        hg_t = sb("hg_t", [P, 4, FB, TS])
        k_t = hg_t[:, :, :, :].rearrange("p n f t -> p (n f t)")[:, 0:4 * G * S].rearrange("p (n g s) -> p n g s", n=4, g=G)
        q_sb = sb("q_sb", [S, 2, H, DH])
        kden = sb("kden", [S, 2, H])
        krec = sb("krec", [S, 2, H])
        qpad = sb("qpad", [S, 2, H, HP])
        q_t = sb("q_t", [P, 2, G, S])
        v_pad = sb("v_pad", [S, 4, H, HP])
        o_pad = sb("o_pad", [P, 2, G, S])
        bo_v = sb("bo_v", [1, C])
        smax = sb("smax", [S, 2, 2, 4])
        orec = sb("orec", [S, 2, H])
        onorm = sb("onorm", [S, 2, H, DH])
        o_t = sb("o_t", [P, 2, S])
        x2 = sb("x2", [S, 2, C])
        x2t = sb("x2t", [P, 2, S])
        BE = B * E
        pick = w_flat[0:S, 0:K * BE].rearrange("s (k b e) -> s k b e", k=K, b=B)
        logits, left, hit = (w_flat[0:S, (K + n) * BE:(K + n + 1) * BE].rearrange("s (b e) -> s b e", b=B)
                             for n in range(3))
        h_flat = hg_t[:, :, :, :].rearrange("p n f t -> p (n f t)")
        chosen = h_flat[0:S, 0:BE].rearrange("s (b e) -> s b e", b=B)
        upto = h_flat[0:S, BE:3 * BE].rearrange("s (n b e) -> s n b e", n=2, b=B)
        top = sb("top", [S, K, B])
        first = sb("first", [S, B])
        zsum = sb("zsum", [S, B])
        zrec = sb("zrec", [S, B])
        gate_v = sb("gate_v", [S, K, B])
        comb = sb("comb", [S, B, EX])
        comb_b = sb("comb_b", [S, 2, EX])
        comb_t = sb("comb_t", [EX, 2, S])
        act_t = sb("act_t", [P, 2, FB, CW])
        zeros = sb("zeros", [P, 4 * C])
        total = sb("total", [S, E])
        tiles_of = sb("tiles_of", [S, E])
        tile_pairs = sb("tile_pairs", [S, E, E])
        tile_at = sb("tile_at", [S, E])
        tile_end = sb("tile_end", [S, E])
        slot_at = sb("slot_at", [S, E])
        slot_f = sb("slot_f", [S, K, B])
        slot_u = ctx.enter_context(nc.sbuf_tensor("slot_u", [S, K, B], mybir.dt.uint32))
        tile_e = sb("tile_e", [1, NT])
        tile_u = ctx.enter_context(nc.sbuf_tensor("tile_u", [1, NT], mybir.dt.int32))
        xg = sb("xg", [P, 4, C])
        xg_t = sb("xg_t", [P, 4, TS])
        yg = sb("yg", [P, 4, C])
        back = act_t[0:S, :, :, :].rearrange("s u f w -> s (u f w)")[:, 0:4 * K * C]\
            .rearrange("s (n k c) -> s n k c", n=4, k=K)
        slots_x = nc.dram_tensor("slots_x", [NT * TS, C], F32, kind="Internal").ap()
        slots_y = nc.dram_tensor("slots_y", [NT * TS, C], F32, kind="Internal").ap()

        ident = wide_sb[:, wide_at["ident"][0]:wide_at["ident"][1]]
        ident_s = ident[0:S, 0:S]
        wk = wide_sb[:, wide_at["wk"][0]:wide_at["wk"][1]].rearrange("p (g c) -> p g c", g=G)
        wqv = wide_sb[:, wide_at["wqv"][0]:wide_at["wqv"][1]]
        wo = wide_sb[:, wide_at["wo"][0]:wide_at["wo"][1]]
        gate_w = wide_sb[:, wide_at["gate"][0]:wide_at["gate"][1]]
        head_of = wide_sb[:, wide_at["head_of"][0]:wide_at["head_of"][1]].rearrange("p (g h) -> p g h", g=G)
        rank = wide_sb[0:S, wide_at["rank"][0]:wide_at["rank"][1]]
        before = wide_sb[0:S, wide_at["before"][0]:wide_at["before"][0] + S]
        every = wide_sb[0:S, wide_at["every"][0]:wide_at["every"][0] + S]
        before_e = wide_sb[0:S, wide_at["before_e"][0]:wide_at["before_e"][1]].rearrange("p (e f) -> p e f", e=E)
        tile_no = rows_sb[0:1, row_at["tile_no"][0]:row_at["tile_no"][1]]
        bq = wide_sb[0:S, wide_at["bq"][0]:wide_at["bq"][1]]
        bo = rows_sb[0:1, row_at["bo"][0]:row_at["bo"][1]]
        ones = rows_sb[0:1, row_at["ones"][0]:row_at["ones"][0] + S]

        def column(name, n=0):
            at = col_at[name][0] + n
            return cols_sb[:, at:at + 1]

        ps = ctx.enter_context(nc.psum_tensor("ps", [P, 8, 512], F32))
        M0, M1 = 6, 7

        frames_in = sem("frames_in")
        tokw_in = sem("tokw_in")
        params_in = sem("params_in")
        w_in = sem("w_in")
        stored = sem("stored")
        pads_zero = sem("pads_zero")
        tok_psum = sem("tok_psum")
        tok_sb = sem("tok_sb")
        tok_stats = sem("tok_stats")
        bn_step = sem("bn_step")
        bn_var = sem("bn_var")
        bn_std = sem("bn_std")
        yt_sb = sem("yt_sb")
        y_psum = sem("y_psum")
        y_sb = sem("y_sb")
        st_step = sem("st_step")
        y_stats = sem("y_stats")
        var1 = sem("var1")
        std1_ok = sem("std1_ok")
        rstd1_ok = sem("rstd1_ok")
        ln_step = sem("ln_step")
        ln_sum = sem("ln_sum")
        h2_kept = sem("h2_kept")
        x_ln = sem("x_ln")
        x_t_psum = sem("x_t_psum")
        x_t_sb = sem("x_t_sb")
        k_psum = sem("k_psum")
        k_sb = sem("k_sb")
        qv_psum = sem("qv_psum")
        qv_sb = sem("qv_sb")
        ks_psum = sem("ks_psum")
        ks_read = sem("ks_read")
        ks_rec = sem("ks_rec")
        q_scaled = sem("q_scaled")
        q_t_psum = sem("q_t_psum")
        q_t_sb = sem("q_t_sb")
        s_psum = sem("s_psum")
        s_max = sem("s_max")
        s_sub = sem("s_sub")
        s_exp = sem("s_exp")
        p_t_psum = sem("p_t_psum")
        p_t_sb = sem("p_t_sb")
        bo_psum = sem("bo_psum")
        bo_sb = sem("bo_sb")
        pv_psum = sem("pv_psum")
        o_low = sem("o_low")
        o_high = sem("o_high")
        o_psum = sem("o_psum")
        o_rec = sem("o_rec")
        o_sb = sem("o_sb")
        o_t_psum = sem("o_t_psum")
        o_t_sb = sem("o_t_sb")
        pr_psum = sem("pr_psum")
        h2_sb = sem("h2_sb")
        h2_st = sem("h2_st")
        h2_mv = sem("h2_mv")
        var2 = sem("var2")
        std2_ok = sem("std2_ok")
        rstd2_ok = sem("rstd2_ok")
        x2_sb = sem("x2_sb")
        x2t_psum = sem("x2t_psum")
        x2t_sb = sem("x2t_sb")
        x2t_kept = sem("x2t_kept")
        lg_psum = sem("lg_psum")
        lg_sb = sem("lg_sb")
        gstep = sem("gstep")
        g_diff = sem("g_diff")
        g_exp = sem("g_exp")
        cb_sb = sem("cb_sb")
        cbt_psum = sem("cbt_psum")
        cbt_sb = sem("cbt_sb")
        b2_psum = sem("b2_psum")
        b2_added = sem("b2_added")
        zero_sb = sem("zero_sb")
        zero_out = sem("zero_out")
        x2_kept = sem("x2_kept")
        chosen_ok = sem("chosen_ok")
        ranks_psum = sem("ranks_psum")
        slots_ok = sem("slots_ok")
        tiles_ok = sem("tiles_ok")
        scattered = sem("scattered")
        xg_in = [sem(f"xg_in{n}") for n in range(4)]
        w_t_sb = sem("w_t_sb")
        xg_psum = sem("xg_psum")
        xg_sb = sem("xg_sb")
        up_psum = sem("up_psum")
        up_sb = sem("up_sb")
        down_psum = sem("down_psum")
        yg_sb = sem("yg_sb")
        yg_out = [sem(f"yg_out{n}") for n in range(4)]
        back_in = [sem(f"back_in{n}") for n in range(4)]
        part = sem("part")
        y_done = sem("y_done")
        f1_psum = sem("f1_psum")
        f1_sb = sem("f1_sb")
        f2_psum = sem("f2_psum")
        f2_added = sem("f2_added")

        def after(eng, s, n, most=B, per=1):
            n = count(n, most)
            if n is not None:
                eng.wait_ge(s, n * per if per != 1 else n)

        def slots(eng, slot):
            lo = 4
            hi = B - 4
            for i in range(-4, lo):
                slot(i, i % 4)
            with eng.Fori(lo, hi - 3, 4) as i:
                for u in range(4):
                    slot(i + u, (lo + u) % 4)
            for i in range(hi, B + 1):
                slot(i, i % 4)

        def lives(b):
            return not isinstance(b, int) or 0 <= b < B

        def pairs(eng, step, lag, lo):
            for i in range(lo):
                step(i, i % 2)
            with eng.Fori(lo, B - 1, 2) as i:
                for u in range(2):
                    step(i + u, u)
            for i in range(B, B + lag):
                step(i, i % 2)

        def slots_of_tiles(eng, slot):
            lo = 4
            hi = lo + (NT - 2 - lo) // 4 * 4
            for i in range(-2, lo):
                slot(i, i % 4)
            with eng.Fori(lo, hi - 3, 4) as i:
                for u in range(4):
                    slot(i + u, u)
            for i in range(hi, NT):
                slot(i, i % 4)

        def has(t):
            return not isinstance(t, int) or 0 <= t < NT

        block = ctx.enter_context(nc.Block())

        @block.sync
        def _(sp):
            for i in range(CTX):
                sp.dma_start(xt_all[i * D:(i + 1) * D, :, :], xT[:, :, i:i + S]).then_inc(frames_in, 16)
            sp.dma_start(wide_sb[:, :], wide).then_inc(params_in, 16)
            sp.dma_start(rows_sb[:, :], rows).then_inc(params_in, 16)
            for e in range(0, E, 4):
                sp.dma_start(w_all[:, e:e + 4, 0:F], re_w1[e:e + 4].rearrange("e h f -> h e f")).then_inc(w_in, 16)
                for c in range(FB):
                    sp.dma_start(w_all[:, e:e + 4, F + FB + c * C:F + FB + (c + 1) * C],
                                 re_w2[e:e + 4, c * P:(c + 1) * P].rearrange("e p h -> p e h")).then_inc(w_in, 16)
            sp.dma_start(w_all[:, :, F:F + FB], re_b1).then_inc(w_in, 16)
            sp.dma_start(w1_sb[:, :, :], se_w1.rearrange("e h f -> h e f")).then_inc(w_in, 16)
            sp.dma_start(w2_sb[:, :, :, :].rearrange("p e c h -> p (e c) h"),
                         se_w2.rearrange("e (c p) h -> p (e c) h", p=P)).then_inc(w_in, 16)
            sp.dma_start(b2_sb[0:E, :], re_b2).then_inc(w_in, 16)
            sp.dma_start(b2_sb[E:EX, :], se_b2).then_inc(w_in, 16)
            sp.wait_ge(zero_sb, 1)
            per = NT * TS * C // P
            sp.dma_start(slots_x.rearrange("(p n) c -> p (n c)", p=P).rearrange("p (r w) -> p r w", w=4 * C),
                         zeros[:, :].unsqueeze(1).broadcast_to([P, per // (4 * C), 4 * C])).then_inc(zero_out, 16)

            sp.wait_ge(scattered, 16 * K * B)

            def load(t, r):
                after(sp, xg_psum, t - 3, NT)
                sp.dma_start(xg[:, r, :], slots_x[bass.ts(t, TS), :]).then_inc(xg_in[r], 16)

            def save(t, r):
                sp.wait_ge(yg_sb, t + 1)
                sp.dma_start(slots_y[bass.ts(t, TS), :], yg[:, r, :]).then_inc(yg_out[r], 16)

            def slot(i, r):
                if has(i + 4) or i < 0:
                    if isinstance(i, int) and i == -2:
                        for t in range(2):
                            load(t, t)
                    load(i + 4, r)
                if has(i):
                    save(i, r)

            lo, hi = 4, 4 + (NT - 4 - 4) // 4 * 4
            for i in range(-2, lo):
                slot(i, i % 4)
            with sp.Fori(lo, hi - 3, 4) as i:
                for u in range(4):
                    slot(i + u, u)
            for i in range(hi, NT):
                slot(i, i % 4)

            with sp.Fori(0, NCH) as c:
                sp.wait_ge(y_done, c * CB + CB)
                sp.dma_start(out.rearrange("b t c -> t b c")[:, bass.ts(c, CB), :],
                             y_all[:, bass.ts(c, CB), :]).then_inc(stored, 16)
            sp.wait_ge(stored, 16 * NCH)

        W_ALL = 16 * (E // 4 * (1 + FB) + 1 + 4)

        @block.gpsimd
        def _(pool):
            nc.gpsimd.memset(qpad[:, :, :, :], 0.0).then_inc(pads_zero, 1)
            nc.gpsimd.memset(v_pad[:, :, :, :], 0.0).then_inc(pads_zero, 1)
            pool.wait_ge(pads_zero, 2)
            nc.gpsimd.memset(v_pad[:, :, :, DH:DH + 1], 1.0).then_inc(pads_zero, 1)
            nc.gpsimd.memset(comb[:, :, :], 1.0 / SH).then_inc(pads_zero, 1)
            nc.gpsimd.memset(zeros[:, :], 0.0).then_inc(zero_sb, 1)

            def keep_h2(b, p):
                pool.wait_ge(h2_sb, b + 1)
                nc.gpsimd.tensor_copy(y_all[:, b, :], h2[:, p, :]).then_inc(h2_kept, 1)

            pairs(pool, keep_h2, 0, 0)

            def step(b, p):
                pool.wait_ge(x2_sb, b + 1)
                nc.gpsimd.tensor_copy(x2_all[:, b, :], x2[:, p, :]).then_inc(x2_kept, 1)
                pool.wait_ge(x2t_sb, b + 1)
                nc.gpsimd.tensor_copy(xt_all[:, b, :], x2t[:, p, :]).then_inc(x2t_kept, 1)

            pairs(pool, step, 0, 0)

            pool.wait_ge(x2_kept, B)
            pool.wait_ge(zero_out, 16)
            pool.wait_ge(slots_ok, 1)
            for b in range(B):
                for k in range(K):
                    pool.indirect_dma_start(slots_x, bass.IndirectOffsetOnAxis(ap=slot_u[:, k, b:b + 1], axis=0),
                                            x2_all[:, b, :], None).then_inc(scattered, 16)
            for r in range(4):
                pool.wait_ge(yg_out[r], 16 * ((NT - r + 3) // 4))
            for b in range(B):
                if b >= 4:
                    pool.wait_ge(y_done, b - 3)
                for k in range(K):
                    pool.indirect_dma_start(back[:, b % 4, k, :], None, slots_y,
                                            bass.IndirectOffsetOnAxis(ap=slot_u[:, k, b:b + 1], axis=0))\
                        .then_inc(back_in[b % 4], 16)

        @block.tensor
        def _(pe):
            pe.wait_ge(frames_in, 16 * CTX)
            pe.wait_ge(tokw_in, 32)

            def tok_chunk(c, p):
                after(pe, tok_sb, c - 1, NCH)
                nc.tensor.matmul(ps[:, p, 0:CW], tokw_sb[:, :], xt_all[0:CTX * D, bass.ts(c, CB), :],
                                 start=True, stop=True).then_inc(tok_psum, 1)

            tok_chunk(0, 0)
            tok_chunk(1, 1)
            with pe.Fori(2, NCH - 1, 2) as c:
                tok_chunk(c, 0)
                tok_chunk(c + 1, 1)

            pe.wait_ge(params_in, 32)

            def turn_y(b, p):
                pe.wait_ge(yt_sb, b + 1)
                after(pe, st_step, b - 1)
                nc.tensor.transpose(ps[0:S, 2 + p, 0:C], yt[:, p, :], ident).then_inc(y_psum, 1)

            pairs(pe, turn_y, 0, 2)

            nc.tensor.matmul(ps[0:1, M1, 0:C], column("bv"), wo, start=True, stop=False)
            nc.tensor.matmul(ps[0:1, M1, 0:C], ones[0:1, 0:1], bo, start=False, stop=True).then_inc(bo_psum, 1)
            pe.wait_ge(bo_sb, 1)

            def slot(i, r):
                steady = not isinstance(i, int)

                def m0_free(x, o, k, q):
                    for s, n, per in ((x_t_sb, x, 1), (o_t_sb, o, 1), (k_sb, k, G), (q_t_sb, q, 1)):
                        if n is not None:
                            after(pe, s, n, per=per)

                def m1_free(ks, pr, qv, o):
                    for s, n, per in ((ks_read, ks, 1), (h2_sb, pr, 1), (qv_sb, qv, 2), (o_sb, o, 1)):
                        if n is not None:
                            after(pe, s, n, per=per)

                def scores(half):
                    b = i + 1
                    if not lives(b):
                        return
                    if half == 0:
                        pe.wait_ge(q_t_sb, b + 1)
                    after(pe, s_sub, 2 * b - 1 + half, 2 * B)
                    for j in (2 * half, 2 * half + 1):
                        for g in range(G):
                            rows_j = slice(HP * j, HP * j + HP)
                            mm = nc.tensor.matmul(ps[0:S, j, g * S:(g + 1) * S], q_t[rows_j, (r + 1) % 2, g, :],
                                                  k_t[rows_j, (r + 1) % 4, g, :], start=True, stop=True)
                    mm.then_inc(s_psum, 1)

                def turn_prob(half):
                    b = i
                    if not lives(b):
                        return
                    pe.wait_ge(s_exp, 2 * b + half + 1)
                    after(pe, o_low, b)
                    after(pe, o_high, b)
                    for n in range(4):
                        mm = nc.tensor.transpose(ps[0:S, 4 + half, n * S:(n + 1) * S],
                                                 prob[:, r % 2, half, n, :], ident_s)
                    mm.then_inc(p_t_psum, 1)

                scores(0)
                if lives(i + 3):
                    b = i + 3
                    pe.wait_ge(x_ln, b + 1)
                    m0_free(*((None, None, None, b - 1) if steady else (b, b - 4, b, b - 1)))
                    nc.tensor.transpose(ps[:, M0, 0:S], xln[:, (r + 3) % 2, :], ident_s).then_inc(x_t_psum, 1)
                scores(1)
                if lives(i - 1):
                    b = i - 1
                    pe.wait_ge(o_low, b + 1)
                    pe.wait_ge(o_high, b + 1)
                    m1_free(*((None, None, b + 4, None) if steady else (b + 3, b, b + 4, b)))
                    for g in range(G):
                        mm = nc.tensor.transpose(ps[0:S, M1, g * P:(g + 1) * P], o_pad[:, (r + 3) % 2, g, :], ident)
                    mm.then_inc(o_psum, 1)
                if lives(i + 3):
                    b = i + 3
                    pe.wait_ge(x_t_sb, b + 1)
                    m0_free(*((None, None, None, None) if steady else (b + 1, b - 4, b, b - 1)))
                    for g in range(G):
                        mm = nc.tensor.matmul(ps[:, M0, g * S:(g + 1) * S], wk[:, g, :], xlnt[:, (r + 3) % 2, :],
                                              start=True, stop=True)
                    mm.then_inc(k_psum, 1)
                turn_prob(0)
                turn_prob(1)
                if lives(i - 1):
                    b = i - 1
                    pe.wait_ge(o_sb, b + 1)
                    m0_free(*((None, None, b + 5, None) if steady else (b + 5, b, b + 5, b + 3)))
                    nc.tensor.transpose(ps[:, M0, 0:S], onorm[:, (r + 3) % 2, :, :].rearrange("s h d -> s (h d)"),
                                        ident_s).then_inc(o_t_psum, 1)
                if lives(i + 2):
                    b = i + 2
                    after(pe, k_sb, b + 1, per=G)
                    m1_free(*((None, None, None, b - 2) if steady else (b, b - 3, b + 1, b - 2)))
                    for g in range(G):
                        mm = nc.tensor.matmul(ps[0:S, M1, 256:256 + H], k_t[:, (r + 2) % 4, g, :], head_of[:, g, :],
                                              start=(g == 0), stop=(g == G - 1))
                    mm.then_inc(ks_psum, 1)
                if lives(i):
                    b = i
                    pe.wait_ge(p_t_sb, 2 * b + 2)
                    probs = prob_t[:, r % 2, :, :, :].rearrange("s h (j g) t -> s g (h j) t", g=G)
                    for g in range(G):
                        mm = nc.tensor.matmul(ps[:, 4 + g, 0:4 * S],
                                              v_pad[:, r, 4 * g:4 * g + 4, :].rearrange("s h d -> s (h d)"),
                                              probs[:, g, :, :], start=True, stop=True)
                    mm.then_inc(pv_psum, 1)
                if lives(i + 2):
                    b = i + 2
                    pe.wait_ge(q_scaled, b + 1)
                    m0_free(*((None, b - 2, None, None) if steady else (b + 2, b - 2, b + 2, b)))
                    for g in range(G):
                        mm = nc.tensor.transpose(ps[:, M0, g * S:(g + 1) * S],
                                                 qpad[:, r % 2, g * 4:(g + 1) * 4, :].rearrange("s h d -> s (h d)"),
                                                 ident_s)
                    mm.then_inc(q_t_psum, 1)
                if lives(i - 1):
                    b = i - 1
                    pe.wait_ge(o_t_sb, b + 1)
                    m1_free(*((b + 4, None, None, None) if steady else (b + 4, b, b + 4, b + 1)))
                    nc.tensor.matmul(ps[0:S, M1, 0:C], ones, bo_v[:, :], start=True, stop=False)
                    nc.tensor.matmul(ps[0:S, M1, 0:C], o_t[:, (r + 3) % 2, :], wo,
                                     start=False, stop=True).then_inc(pr_psum, 1)
                if lives(i + 3):
                    b = i + 3
                    m1_free(*((None, b - 3, None, None) if steady else (b, b - 3, b, b - 3)))
                    nc.tensor.matmul(ps[0:S, M1, 0:2 * C], xlnt[:, (r + 3) % 2, :], wqv,
                                     start=True, stop=True).then_inc(qv_psum, 1)

            slots(pe, slot)

            def gate_step(b, p):
                if lives(b):
                    pe.wait_ge(x2_sb, b + 1)
                    after(pe, x2t_sb, b - 1)
                    nc.tensor.transpose(ps[:, p, 0:S], x2[:, p, :], ident_s).then_inc(x2t_psum, 1)
                if lives(b - 1):
                    pe.wait_ge(x2t_sb, b)
                    after(pe, lg_sb, b - 2)
                    nc.tensor.matmul(ps[0:S, 3 - p, 0:E], x2t[:, 1 - p, :], gate_w,
                                     start=True, stop=True).then_inc(lg_psum, 1)

            pairs(pe, gate_step, 1, 4)

            pe.wait_ge(chosen_ok, 1)
            flat = chosen[:, :, :].rearrange("s b e -> s (b e)")
            nc.tensor.matmul(ps[0:S, 6, 0:B * E], before, flat, start=True, stop=True).then_inc(ranks_psum, 1)
            nc.tensor.matmul(ps[0:S, 7, 0:B * E], every, flat, start=True, stop=True).then_inc(ranks_psum, 1)

            pe.wait_ge(w_in, W_ALL)

            def bias_step(b, p):
                if lives(b):
                    pe.wait_ge(cb_sb, b + 1)
                    after(pe, cbt_sb, b - 1)
                    nc.tensor.transpose(ps[0:EX, 4 + p, 0:S], comb_b[:, p, :], ident_s).then_inc(cbt_psum, 1)
                if lives(b - 1):
                    pe.wait_ge(cbt_sb, b)
                    after(pe, b2_added, b - 2)
                    nc.tensor.matmul(ps[0:S, 7 - p, 0:C], comb_t[:, 1 - p, :], b2_sb[:, :],
                                     start=True, stop=True).then_inc(b2_psum, 1)

            pairs(pe, bias_step, 1, 4)

            pe.wait_ge(x2t_kept, B)
            pe.wait_ge(b2_added, B)

            def up(c, e, n):
                for fb in range(FB):
                    if fb == 0:
                        pass
                    v = count(n * FB + fb + 1 - FB, 10 ** 6)
                    if v is not None:
                        pe.wait_ge(f1_sb, v)
                    nc.tensor.matmul(ps[:, fb, 0:CW], w1_sb[:, e, fb * P:(fb + 1) * P],
                                     xt_all[:, bass.ts(c, CB), :], start=True, stop=True).then_inc(f1_psum, 1)

            def down(n, e):
                pe.wait_ge(f1_sb, n * FB + FB)
                v = count((n - 1) * CB, 10 ** 6)
                if v is not None:
                    pe.wait_ge(f2_added, v)
                for s in range(CB):
                    for fb in range(FB):
                        mm = nc.tensor.matmul(ps[0:S, 4 + e % 2, s * C:(s + 1) * C],
                                              act_t[:, e % 2, fb, s * S:(s + 1) * S], w2_sb[:, e, fb, :],
                                              start=(fb == 0), stop=(fb == FB - 1))
                    mm.then_inc(f2_psum, 1)

            def chunk(c):
                up(c, 0, c * SH)
                for e in range(SH):
                    if e + 1 < SH:
                        up(c, e + 1, c * SH + e + 1)
                    down(c * SH + e, e)

            chunk(0)
            with pe.Fori(1, NCH) as c:
                chunk(c)

            pe.wait_ge(f2_added, NCH * SH * CB)

            def slot(i, r):
                if has(i + 2):
                    t, q = i + 2, (r + 2) % 4
                    pe.wait_ge(xg_in[q], 16 * (t // 4 + 1) if isinstance(t, int) else t * 4 + (16 - 4 * q))
                    after(pe, xg_sb, t - 1, NT)
                    nc.tensor.transpose(ps[:, q % 2, 0:TS], xg[:, q, :], ident).then_inc(xg_psum, 1)
                if has(i + 1):
                    t, q = i + 1, (r + 1) % 4
                    pe.wait_ge(xg_sb, t + 1)
                    pe.wait_ge(w_t_sb, t + 1)
                    after(pe, up_sb, (t - 1), NT)
                    for fb in range(FB):
                        mm = nc.tensor.matmul(ps[:, 2 + q % 2, fb * TS:(fb + 1) * TS], w_t[:, q, fb * P:(fb + 1) * P],
                                              xg_t[:, q, :], start=True, stop=True)
                    mm.then_inc(up_psum, 1)
                if has(i):
                    pe.wait_ge(up_sb, i + 1)
                    after(pe, yg_sb, i - 1, NT)
                    for fb in range(FB):
                        at = F + FB + fb * C
                        mm = nc.tensor.matmul(ps[:, 4 + r % 2, 0:C], hg_t[:, r, fb, :], w_t[:, r, at:at + C],
                                              start=(fb == 0), stop=(fb == FB - 1))
                    mm.then_inc(down_psum, 1)

            slots_of_tiles(pe, slot)

        @block.scalar
        def _(act):
            act.dma_start(tokw_sb[:, :], tok_w).then_inc(tokw_in, 16)
            act.dma_start(cols_sb[:, :], columns).then_inc(tokw_in, 16)
            act.wait_ge(tokw_in, 32)
            with act.Fori(0, NCH - 1, 2) as c0:
                for u in range(2):
                    c = c0 + u
                    act.wait_ge(tok_psum, c + 1)
                    nc.scalar.activation(hid_t[:, bass.ts(c, CB), :].rearrange("p b s -> p (b s)"), ps[:, u, 0:CW],
                                         ACT.Relu, bias=column("tok_b")).then_inc(tok_sb, 1)
            act.wait_ge(bn_var, 1)
            nc.scalar.activation(bn_t[:, 1:2], bn_t[:, 0:1], ACT.Sqrt).then_inc(bn_std, 1)

            def keep_y(b, p):
                act.wait_ge(y_psum, b + 1)
                nc.scalar.copy(y_all[:, b, :], ps[0:S, 2 + p, 0:C]).then_inc(y_sb, 1)

            pairs(act, keep_y, 0, 0)
            act.wait_ge(var1, 1)
            nc.scalar.activation(std1[:, :], rstd1[:, :], ACT.Sqrt).then_inc(std1_ok, 1)
            act.wait_ge(params_in, 32)
            act.wait_ge(bo_psum, 1)
            nc.scalar.copy(bo_v[:, :], ps[0:1, M1, 0:C]).then_inc(bo_sb, 1)

            def slot(i, r):
                def exp(half):
                    b = i + 1
                    if lives(b):
                        act.wait_ge(s_sub, 2 * b + half + 1)
                        x = prob[:, (r + 1) % 2, half, :, :]
                        nc.scalar.activation(x, x, ACT.Exp).then_inc(s_exp, 1)

                def keep_prob_t(half):
                    b = i
                    if lives(b):
                        act.wait_ge(p_t_psum, 2 * b + half + 1)
                        after(act, pv_psum, b - 1)
                        nc.scalar.copy(prob_t[:, r % 2, half, :, :].rearrange("s n t -> s (n t)"),
                                       ps[0:S, 4 + half, 0:4 * S]).then_inc(p_t_sb, 1)

                if lives(i + 3):
                    b = i + 3
                    act.wait_ge(x_t_psum, b + 1)
                    after(act, qv_psum, b - 1)
                    nc.scalar.copy(xlnt[:, (r + 3) % 2, :], ps[:, M0, 0:S]).then_inc(x_t_sb, 1)
                exp(0)
                if lives(i + 3):
                    b = i + 3
                    act.wait_ge(k_psum, b + 1)
                    after(act, s_psum, 2 * b - 6, 2 * B)
                    for g in range(G):
                        nc.scalar.activation(k_t[:, (r + 3) % 4, g, :], ps[:, M0, g * S:(g + 1) * S], ACT.Relu,
                                             bias=column("bk", g)).then_inc(k_sb, 1)
                keep_prob_t(0)
                keep_prob_t(1)
                if lives(i - 1):
                    b = i - 1
                    act.wait_ge(o_t_psum, b + 1)
                    after(act, pr_psum, b - 1)
                    nc.scalar.copy(o_t[:, (r + 3) % 2, :], ps[:, M0, 0:S]).then_inc(o_t_sb, 1)
                exp(1)
                if lives(i):
                    b = i
                    act.wait_ge(pv_psum, b + 1)
                    after(act, o_psum, b - 1)
                    for j in (0, 1):
                        rows_j = slice(HP * j, HP * j + HP)
                        cp = nc.scalar.copy(o_pad[rows_j, r % 2, :, :], ps[rows_j, 4:6, j * S:(j + 1) * S])
                    cp.then_inc(o_low, 1)
                if lives(i + 2):
                    b = i + 2
                    act.wait_ge(q_t_psum, b + 1)
                    after(act, s_psum, 2 * b - 2, 2 * B)
                    nc.scalar.copy(q_t[:, r % 2, :, :].rearrange("p g s -> p (g s)"),
                                   ps[:, M0, 0:G * S]).then_inc(q_t_sb, 1)

            slots(act, slot)
            act.wait_ge(var2, 1)
            nc.scalar.activation(std2[:, :], rstd2[:, :], ACT.Sqrt).then_inc(std2_ok, 1)

            def keep_x2t(b, p):
                act.wait_ge(x2t_psum, b + 1)
                after(act, lg_psum, b - 1)
                after(act, x2t_kept, b - 1)
                nc.scalar.copy(x2t[:, p, :], ps[:, p, 0:S]).then_inc(x2t_sb, 1)

            pairs(act, keep_x2t, 0, 2)

            act.wait_ge(g_diff, 2)
            nc.scalar.activation(left[:, :, :], left[:, :, :], ACT.Exp).then_inc(g_exp, 1)
            nc.scalar.activation(gate_v[:, :, :], gate_v[:, :, :], ACT.Exp).then_inc(g_exp, 1)
            act.wait_ge(g_diff, 3)
            nc.scalar.activation(gate_v[:, :, :], gate_v[:, :, :], ACT.Exp).then_inc(g_exp, 1)

            def keep_comb_t(b, p):
                act.wait_ge(cbt_psum, b + 1)
                after(act, b2_psum, b - 1)
                nc.scalar.copy(comb_t[:, p, :], ps[0:EX, 4 + p, 0:S]).then_inc(cbt_sb, 1)

            pairs(act, keep_comb_t, 0, 2)

            def chunk(c):
                for e in range(SH):
                    n = c * SH + e
                    v = count((n - 1) * CB, 10 ** 6)
                    if v is not None:
                        act.wait_ge(f2_psum, v)
                    for fb in range(FB):
                        act.wait_ge(f1_psum, n * FB + fb + 1)
                        nc.scalar.activation(act_t[:, e % 2, fb, :], ps[:, fb, 0:CW], ACT.Gelu,
                                             bias=column("b1", e * FB + fb)).then_inc(f1_sb, 1)

            chunk(0)
            with act.Fori(1, NCH) as c:
                chunk(c)

            def slot(i, r):
                if has(i + 1):
                    t, q = i + 1, (r + 1) % 4
                    act.wait_ge(up_psum, t + 1)
                    after(act, down_psum, t - 3, NT)
                    for fb in range(FB):
                        g = nc.scalar.activation(hg_t[:, q, fb, :], ps[:, 2 + q % 2, fb * TS:(fb + 1) * TS], ACT.Gelu,
                                                 bias=w_t[:, q, F + fb:F + fb + 1])
                    g.then_inc(up_sb, 1)

            slots_of_tiles(act, slot)

        @block.vector
        def _(dve):
            v = nc.vector
            dve.wait_ge(tokw_in, 32)
            for c in range(NCH):
                dve.wait_ge(tok_sb, c + 1)
                v.bn_stats(bn_st[:, c, :], hid_t[:, c * CB:(c + 1) * CB, :].rearrange("p b s -> p (b s)"))\
                 .then_inc(tok_stats, 1)
            dve.wait_ge(tok_stats, NCH)
            v.bn_aggr(bn_mv[:, :], bn_st[:, :, :]).then_inc(bn_step, 1)
            dve.wait_ge(bn_step, 1)
            v.tensor_scalar(bn_t[:, 0:1], bn_mv[:, 1:2], BN_EPS, None, ALU.add).then_inc(bn_var, 1)
            dve.wait_ge(bn_std, 1)
            v.reciprocal(bn_t[:, 2:3], bn_t[:, 1:2]).then_inc(bn_step, 1)
            dve.wait_ge(bn_step, 2)
            v.tensor_tensor(bn_t[:, 2:3], bn_t[:, 2:3], column("tok_gamma"), ALU.mult).then_inc(bn_step, 1)
            dve.wait_ge(bn_step, 3)
            v.scalar_tensor_tensor(bn_t[:, 3:4], bn_mv[:, 0:1], bn_t[:, 2:3], column("tok_beta"),
                                   ALU.mult, ALU.subtract).then_inc(bn_step, 1)
            dve.wait_ge(bn_step, 4)

            def join_stats(mean, var, done, ready):
                v.tensor_tensor(mean[:, :], st_all[:, :, 1], st_all[:, :, 4], ALU.add).then_inc(ln_step, 1)
                v.tensor_tensor(half_gap[:, :], st_all[:, :, 1], st_all[:, :, 4], ALU.subtract).then_inc(ln_step, 1)
                dve.wait_ge(ln_step, done + 2)
                v.tensor_scalar(mean[:, :], mean[:, :], 0.5, None, ALU.mult).then_inc(ln_step, 1)
                v.scalar_tensor_tensor(half_gap[:, :], half_gap[:, :], 0.25 * C, half_gap[:, :],
                                       ALU.mult, ALU.mult).then_inc(ln_step, 1)
                dve.wait_ge(ln_step, done + 4)
                v.tensor_tensor(var[:, :], st_all[:, :, 2], st_all[:, :, 5], ALU.add).then_inc(ln_sum, 1)
                dve.wait_ge(ln_sum, done // 2 + 1)
                v.tensor_tensor(var[:, :], var[:, :], half_gap[:, :], ALU.add).then_inc(ln_sum, 1)
                dve.wait_ge(ln_sum, done // 2 + 2)
                v.tensor_scalar(var[:, :], var[:, :], 1.0 / C, LN_EPS, ALU.mult, ALU.add).then_inc(ready, 1)

            def y_step(b, p):
                if lives(b):
                    after(dve, y_psum, b - 1)
                    v.tensor_scalar(yt[:, p, :], hid_t[:, b, :], bn_t[:, 2:3], bn_t[:, 3:4],
                                    ALU.mult, ALU.subtract).then_inc(yt_sb, 1)
                if lives(b - 2):
                    d = b - 2
                    dve.wait_ge(y_sb, d + 1)
                    after(dve, y_stats, d - 1)
                    v.bn_stats(ln_st[:, p, :], ps[0:S, 2 + p, 0:C]).then_inc(st_step, 1)
                    dve.wait_ge(st_step, d + 1)
                    v.tensor_copy(st_all[:, d, :], ln_st[:, p, :]).then_inc(y_stats, 1)

            pairs(dve, y_step, 2, 4)
            dve.wait_ge(y_stats, B)
            join_stats(mean1, rstd1, 0, var1)
            dve.wait_ge(std1_ok, 1)
            v.reciprocal(rstd1[:, :], std1[:, :]).then_inc(rstd1_ok, 1)
            dve.wait_ge(rstd1_ok, 1)
            dve.wait_ge(pads_zero, 4)

            def slot(i, r):
                def row_max(half):
                    b = i + 1
                    if not lives(b):
                        return
                    dve.wait_ge(s_psum, 2 * b + half + 1)
                    after(dve, p_t_psum, 2 * b - 3 + half, 2 * B)
                    scores = ps[0:S, 2 * half:2 * half + 2, 0:G * S].rearrange("s j (g t) -> s j g t", g=G)
                    top4 = smax[:, (r + 1) % 2, half, :].rearrange("s (j g) -> s j g", g=G)
                    v.tensor_reduce(top4, scores, AX.X, ALU.max).then_inc(s_max, 1)
                    dve.wait_ge(s_max, 2 * b + half + 1)
                    v.tensor_tensor(prob[:, (r + 1) % 2, half, :, :].rearrange("s (j g) t -> s j g t", g=G), scores,
                                    top4.unsqueeze(3).broadcast_to([S, 2, G, S]), ALU.subtract).then_inc(s_sub, 1)

                row_max(0)
                if lives(i - 1):
                    b = i - 1
                    dve.wait_ge(o_psum, b + 1)
                    o = ps[0:S, M1, 0:H * HP].rearrange("s (h d) -> s h d", d=HP)
                    v.reciprocal(orec[:, (r + 3) % 2, :], o[:, :, DH]).then_inc(o_rec, 1)
                    dve.wait_ge(o_rec, b + 1)
                    after(dve, o_t_psum, b - 1)
                    v.tensor_tensor(onorm[:, (r + 3) % 2, :, :], o[:, :, 0:DH],
                                    orec[:, (r + 3) % 2, :].unsqueeze(2).broadcast_to([S, H, DH]),
                                    ALU.mult).then_inc(o_sb, 1)
                row_max(1)
                if lives(i + 2):
                    b = i + 2
                    dve.wait_ge(ks_psum, b + 1)
                    v.tensor_scalar(kden[:, r % 2, :], ps[0:S, M1, 256:256 + H], ATT_EPS, None,
                                    ALU.add).then_inc(ks_read, 1)
                    dve.wait_ge(ks_read, b + 1)
                    v.reciprocal(krec[:, r % 2, :], kden[:, r % 2, :]).then_inc(ks_rec, 1)
                    dve.wait_ge(ks_rec, b + 1)
                    dve.wait_ge(qv_sb, 2 * b + 2)
                    after(dve, q_t_psum, b - 1)
                    v.scalar_tensor_tensor(qpad[:, r % 2, :, 0:DH], q_sb[:, r % 2, :, :], 0.0,
                                           krec[:, r % 2, :].unsqueeze(2).broadcast_to([S, H, DH]),
                                           ALU.max, ALU.mult).then_inc(q_scaled, 1)
                if lives(i):
                    b = i
                    dve.wait_ge(pv_psum, b + 1)
                    after(dve, o_psum, b - 1)
                    for j in (2, 3):
                        rows_j = slice(HP * j, HP * j + HP)
                        cp = v.tensor_copy(o_pad[rows_j, r % 2, :, :], ps[rows_j, 4:6, j * S:(j + 1) * S])
                    cp.then_inc(o_high, 1)
                if lives(i - 1):
                    b = i - 1
                    dve.wait_ge(pr_psum, b + 1)
                    after(dve, h2_kept, b - 1)
                    v.tensor_tensor(h2[:, (r + 3) % 2, :], ps[0:S, M1, 0:C], y_all[:, b, :],
                                    ALU.add).then_inc(h2_sb, 1)
                    dve.wait_ge(h2_sb, b + 1)
                    v.bn_stats(ln_st[:, (r + 3) % 2, :], h2[:, (r + 3) % 2, :]).then_inc(h2_st, 1)
                    dve.wait_ge(h2_st, b + 1)
                    v.tensor_copy(st_all[:, b, :], ln_st[:, (r + 3) % 2, :]).then_inc(h2_mv, 1)
                if lives(i + 4):
                    b = i + 4
                    after(dve, x_t_psum, b - 1)
                    v.tensor_scalar(xln[:, r % 2, :], y_all[:, b, :], mean1[:, bass.ds(b, 1)],
                                    rstd1[:, bass.ds(b, 1)], ALU.subtract, ALU.mult).then_inc(x_ln, 1)
                if lives(i + 3):
                    b = i + 3
                    dve.wait_ge(qv_psum, b + 1)
                    after(dve, q_scaled, b - 1)
                    v.tensor_tensor(q_sb[:, (r + 3) % 2, :, :].rearrange("s h d -> s (h d)"), ps[0:S, M1, 0:C], bq,
                                    ALU.add).then_inc(qv_sb, 1)
                    after(dve, pv_psum, b - 3)
                    v.tensor_copy(v_pad[:, (r + 3) % 4, :, 0:DH],
                                  ps[0:S, M1, C:2 * C].rearrange("s (h d) -> s h d", d=DH)).then_inc(qv_sb, 1)

            slots(dve, slot)
            dve.wait_ge(h2_mv, B)
            dve.wait_ge(h2_kept, B)
            join_stats(mean2, rstd2, 4, var2)
            dve.wait_ge(std2_ok, 1)
            v.reciprocal(rstd2[:, :], std2[:, :]).then_inc(rstd2_ok, 1)
            dve.wait_ge(rstd2_ok, 1)

            def gate_step(b, p):
                if lives(b):
                    after(dve, x2t_psum, b - 1)
                    after(dve, x2_kept, b - 1)
                    v.tensor_scalar(x2[:, p, :], y_all[:, b, :], mean2[:, bass.ds(b, 1)], rstd2[:, bass.ds(b, 1)],
                                    ALU.subtract, ALU.mult).then_inc(x2_sb, 1)
                if lives(b - 2):
                    dve.wait_ge(lg_psum, b - 1)
                    v.tensor_copy(logits[:, b - 2, :], ps[0:S, 2 + p, 0:E]).then_inc(lg_sb, 1)

            pairs(dve, gate_step, 2, 4)
            dve.wait_ge(lg_sb, B)

            steps = [0]

            def then(ins):
                steps[0] += 1
                ins.then_inc(gstep, 1)
                dve.wait_ge(gstep, steps[0])

            wide3 = [S, B, E]
            def slots_of_tokens():
                dve.wait_ge(ranks_psum, 2)
                cnt = ps[0:S, 7, 0:B * E].rearrange("s (b e) -> s b e", e=E)
                rank_in = ps[0:S, 6, 0:B * E].rearrange("s (b e) -> s b e", e=E)
                then(v.tensor_copy(upto[:, 0, :, :], cnt))
                a, d = 0, 1
                while d < B:
                    then(v.tensor_tensor(upto[:, 1 - a, d:B, :], upto[:, a, d:B, :], upto[:, a, 0:B - d, :], ALU.add))
                    then(v.tensor_copy(upto[:, 1 - a, 0:d, :], upto[:, a, 0:d, :]))
                    a, d = 1 - a, 2 * d
                then(v.tensor_scalar(total[:, :], upto[:, a, B - 1, :], 1.0 / TS, (TS - 1) / (2.0 * TS),
                                     ALU.mult, ALU.add))
                then(v.tensor_scalar(total[:, :], total[:, :], MAGIC, None, ALU.add))
                then(v.tensor_scalar(tiles_of[:, :], total[:, :], MAGIC, None, ALU.subtract))
                then(v.tensor_tensor(tile_pairs[:, :, :], before_e, tiles_of[:, :].unsqueeze(1).broadcast_to([S, E, E]),
                                     ALU.mult))
                then(v.tensor_reduce(tile_at[:, :], tile_pairs[:, :, :], AX.X, ALU.add))
                then(v.tensor_tensor(tile_end[:, :], tile_at[:, :], tiles_of[:, :], ALU.add))
                then(v.tensor_scalar(slot_at[:, :], tile_at[:, :], float(TS), None, ALU.mult))
                o = 1 - a
                then(v.tensor_tensor(upto[:, o, :, :], upto[:, a, :, :], cnt, ALU.subtract))
                then(v.tensor_tensor(upto[:, o, :, :], upto[:, o, :, :], rank_in, ALU.add))
                then(v.tensor_tensor(upto[:, o, :, :], upto[:, o, :, :],
                                     slot_at[:, :].unsqueeze(1).broadcast_to([S, B, E]), ALU.add))
                for k in range(K):
                    then(v.tensor_tensor(hit[:, :, :], pick[:, k, :, :], upto[:, o, :, :], ALU.mult))
                    then(v.tensor_reduce(slot_f[:, k, :], hit[:, :, :], AX.X, ALU.add))
                v.tensor_copy(slot_u[:, :, :], slot_f[:, :, :]).then_inc(slots_ok, 1)
                ended = act_t[0:1, :, :, :].rearrange("o u f w -> o (u f w)")[:, 0:NT * E]\
                    .rearrange("o (t e) -> o t e", e=E)
                then(v.tensor_tensor(ended, tile_end[0:1, :].unsqueeze(1).broadcast_to([1, NT, E]),
                                     tile_no.unsqueeze(2).broadcast_to([1, NT, E]), ALU.is_le))
                then(v.tensor_reduce(tile_e[:, :], ended, AX.X, ALU.add))
                v.tensor_scalar(tile_u[:, :], tile_e[:, :], float(E - 1), None, ALU.min).then_inc(tiles_ok, 1)
                dve.wait_ge(tiles_ok, 1)

            then(v.tensor_copy(left[:, :, :], logits[:, :, :]))
            for k in range(K):
                then(v.tensor_reduce(top[:, k, :], left[:, :, :], AX.X, ALU.max))
                then(v.tensor_tensor(hit[:, :, :], left[:, :, :], top[:, k, :].unsqueeze(2).broadcast_to(wide3),
                                     ALU.is_ge))
                then(v.tensor_tensor(hit[:, :, :], hit[:, :, :], rank.unsqueeze(1).broadcast_to(wide3), ALU.mult))
                then(v.tensor_reduce(first[:, :], hit[:, :, :], AX.X, ALU.max))
                then(v.tensor_tensor(pick[:, k, :, :], hit[:, :, :], first[:, :].unsqueeze(2).broadcast_to(wide3),
                                     ALU.is_equal))
                then(v.scalar_tensor_tensor(left[:, :, :], pick[:, k, :, :], -3.0e38, left[:, :, :],
                                            ALU.mult, ALU.add))
            then(v.tensor_tensor(chosen[:, :, :], pick[:, 0, :, :], pick[:, 1, :, :], ALU.add))
            then(v.tensor_tensor(chosen[:, :, :], chosen[:, :, :], pick[:, 2, :, :], ALU.add))
            v.tensor_tensor(chosen[:, :, :], chosen[:, :, :], pick[:, 3, :, :], ALU.add).then_inc(chosen_ok, 1)
            v.tensor_tensor(left[:, :, :], logits[:, :, :], top[:, 0, :].unsqueeze(2).broadcast_to(wide3),
                            ALU.subtract).then_inc(g_diff, 1)
            v.tensor_tensor(gate_v[:, :, :], top[:, :, :], top[:, 0, :].unsqueeze(1).broadcast_to([S, K, B]),
                            ALU.subtract).then_inc(g_diff, 1)
            dve.wait_ge(g_exp, 2)
            then(v.tensor_reduce(zsum[:, :], left[:, :, :], AX.X, ALU.add))
            then(v.reciprocal(zrec[:, :], zsum[:, :]))
            then(v.tensor_tensor(gate_v[:, :, :], gate_v[:, :, :], zrec[:, :].unsqueeze(1).broadcast_to([S, K, B]),
                                 ALU.mult))
            then(v.tensor_copy(first[:, :], gate_v[:, 0, :]))
            v.tensor_tensor(gate_v[:, :, :], gate_v[:, :, :], first[:, :].unsqueeze(1).broadcast_to([S, K, B]),
                            ALU.subtract).then_inc(g_diff, 1)
            dve.wait_ge(g_exp, 3)
            then(v.tensor_reduce(zsum[:, :], gate_v[:, :, :].rearrange("s k b -> s b k"), AX.X, ALU.add))
            then(v.reciprocal(zrec[:, :], zsum[:, :]))
            then(v.tensor_tensor(gate_v[:, :, :], gate_v[:, :, :], zrec[:, :].unsqueeze(1).broadcast_to([S, K, B]),
                                 ALU.mult))
            for k in range(K):
                dst = comb[:, :, 0:E] if k == 0 else hit[:, :, :]
                then(v.tensor_tensor(dst, pick[:, k, :, :], gate_v[:, k, :].unsqueeze(2).broadcast_to(wide3), ALU.mult))
                if k:
                    then(v.tensor_tensor(comb[:, :, 0:E], comb[:, :, 0:E], hit[:, :, :], ALU.add))

            slots_of_tokens()

            def bias_step(b, p):
                if lives(b):
                    after(dve, cbt_psum, b - 1)
                    v.tensor_copy(comb_b[:, p, :], comb[:, b, :]).then_inc(cb_sb, 1)
                if lives(b - 2):
                    d = b - 2
                    dve.wait_ge(b2_psum, d + 1)
                    v.tensor_tensor(y_all[:, d, :], ps[0:S, 6 + p, 0:C], y_all[:, d, :], ALU.add).then_inc(b2_added, 1)

            pairs(dve, bias_step, 2, 4)
            dve.wait_ge(b2_added, B)

            def chunk(c):
                for e in range(SH):
                    n = c * SH + e
                    dve.wait_ge(f2_psum, n * CB + CB)
                    if e:
                        dve.wait_ge(f2_added, n * CB)
                    for s in range(CB):
                        b = c * CB + s
                        v.scalar_tensor_tensor(y_all[:, b, :], ps[0:S, 4 + e % 2, s * C:(s + 1) * C],
                                               1.0 / SH, y_all[:, b, :],
                                               ALU.mult, ALU.add).then_inc(f2_added, 1)

            chunk(0)
            with dve.Fori(1, NCH) as c:
                chunk(c)

            def slot(i, r):
                if has(i + 2):
                    t, q = i + 2, (r + 2) % 4
                    e = dve.value_load(tile_u[0:1, bass.ds(t, 1)], min_val=0, max_val=E - 1)
                    after(dve, down_psum, t - 3, NT)
                    v.tensor_copy(w_t[:, q, :], w_all[:, e, :]).then_inc(w_t_sb, 1)
                    dve.wait_ge(xg_psum, t + 1)
                    after(dve, up_psum, t - 3, NT)
                    v.tensor_copy(xg_t[:, q, :], ps[:, q % 2, 0:TS]).then_inc(xg_sb, 1)
                if has(i):
                    dve.wait_ge(down_psum, i + 1)
                    if not (isinstance(i, int) and i < 4):
                        dve.wait_ge(yg_out[r], 16 * (i // 4) if isinstance(i, int) else i * 4 - 4 * r)
                    v.tensor_copy(yg[:, r, :], ps[:, 4 + r % 2, 0:C]).then_inc(yg_sb, 1)

            slots_of_tiles(dve, slot)

            def combine(b, r):
                dve.wait_ge(back_in[r], 16 * b + (64 - 16 * r))
                for k in range(K):
                    ins = v.scalar_tensor_tensor(y_all[:, b, :], back[:, r, k, :], gate_v[:, k, bass.ds(b, 1)],
                                                 y_all[:, b, :], ALU.mult, ALU.add)
                    if k < K - 1:
                        ins.then_inc(part, 1)
                        dve.wait_ge(part, b * (K - 1) + (k + 1))
                    else:
                        ins.then_inc(y_done, 1)

            with dve.Fori(0, B - 3, 4) as b:
                for u in range(4):
                    combine(b + u, u)


def kernel(**inputs):
    import numpy as np
    import concourse.bacc as bacc
    from concourse import mybir as mb
    from concourse.bass_utils import run_bass_kernel_spmd

    a = {k: np.asarray(v) for k, v in inputs.items()}
    H, DH = 8, 16
    C = a["L0_tok_W"].shape[0]
    E, _, F = a["L0_ffn_re_w1"].shape
    B, T, D = a["x"].shape
    f32 = np.float32

    def padded_heads(w):
        o = np.zeros(w.shape[:-1] + (H, 2 * DH), f32)
        o[..., :DH] = w.reshape(w.shape[:-1] + (H, DH))
        return o.reshape(w.shape[:-1] + (2 * H * DH,))

    head_of = np.zeros((2, P, H), f32)
    for h in range(H):
        head_of[h // 4, 32 * (h % 4):32 * (h % 4) + DH, h] = 1.0
    b1 = a["L0_ffn_se_b1"].reshape(-1, P).T
    re_b1 = a["L0_ffn_re_b1"].reshape(E, F // P, P).transpose(2, 0, 1)
    columns = np.concatenate([a["L0_tok_b"][:, None], a["L0_tok_gamma"][:, None], a["L0_tok_beta"][:, None],
                              padded_heads(a["L0_attn_bk"]).reshape(2, P).T, b1, a["L0_attn_bv"][:, None]], axis=1)
    wide = np.concatenate([padded_heads(a["L0_attn_Wk"].T), a["L0_attn_Wq"].T, a["L0_attn_Wv"].T, a["L0_attn_Wo"].T,
                           a["L0_ffn_gate_w"].T, np.eye(P, dtype=f32),
                           head_of.transpose(1, 0, 2).reshape(P, 2 * H),
                           np.broadcast_to(np.arange(E, 0, -1, dtype=f32), (P, E)),
                           np.triu(np.ones((P, P), f32), 1), np.ones((P, P), f32),
                           np.broadcast_to(np.tril(np.ones((E, E), f32), -1).reshape(1, -1), (P, E * E)),
                           np.broadcast_to(a["L0_attn_bq"], (P, C))], axis=1)
    rows = np.concatenate([a["L0_attn_bo"], np.ones(P, f32),
                           np.arange(136, dtype=f32)])[None, :]
    arrays = {"xT": a["x"].transpose(2, 0, 1), "tok_w": a["L0_tok_W"].T, "columns": columns, "wide": wide,
              "rows": rows, "re_w1": a["L0_ffn_re_w1"], "re_w2": a["L0_ffn_re_w2"], "se_w1": a["L0_ffn_se_w1"],
              "se_w2": a["L0_ffn_se_w2"], "re_b2": a["L0_ffn_re_b2"], "se_b2": a["L0_ffn_se_b2"], "re_b1": re_b1}
    arrays = {k: np.ascontiguousarray(v) for k, v in arrays.items()}

    nc = bacc.Bacc("TRN2", target_bir_lowering=False, num_devices=1)
    args = [nc.dram_tensor(k, v.shape, mb.dt.from_np(v.dtype), kind="ExternalInput").ap() for k, v in arrays.items()]
    S = T - a["L0_tok_W"].shape[1] // D + 1
    args.append(nc.dram_tensor("y", (B, S, C), mb.dt.float32, kind="ExternalOutput").ap())
    build(nc, *args)
    return run_bass_kernel_spmd(nc, [arrays], core_ids=[0]).results[0]["y"]
```

```python
from contextlib import ExitStack

import concourse.bass as bass
from concourse import mybir

P = 128
F32 = mybir.dt.float32
ALU = mybir.AluOpType
ACT = mybir.ActivationFunctionType
AX = mybir.AxisListType

COLUMNS = [("tok_b", 1), ("tok_gamma", 1), ("tok_beta", 1), ("bk", 2), ("b1", 8), ("bv", 1)]
WIDE = [("wk", 256), ("wqv", 256), ("wo", 128), ("gate", 16), ("ident", 128), ("head_of", 16),
        ("before", 128), ("every", 128), ("before_e", 256), ("bq", 128), ("numbers", 136), ("item_no", 128),
        ("spare_no", 136), ("difference", 128)]
ROWS = [("bo", 128), ("ones", 128)]


def spans(groups):
    at, out = 0, {}
    for name, width in groups:
        out[name] = (at, at + width)
        at += width
    return out, at


def count(n, most):
    if isinstance(n, int):
        return None if n <= 0 else min(n, most)
    return n


def build(nc, xT, tok_w, columns, wide, rows, re_w1, re_w2, se_w1, se_w2, re_b2, se_b2, re_b1, out):
    D, B, T = xT.shape
    CTX = tok_w.shape[0] // D
    S = T - CTX + 1
    C = tok_w.shape[1]
    H, DH = 8, 16
    HP = 2 * DH
    G = H * HP // P
    E, _, F = re_w1.shape
    SH = se_w1.shape[0]
    EX = E + SH
    FB = F // P
    K = 4
    CB = 4
    NCH = B // CB
    QR = P // CB
    CW = CB * S
    N = B * S
    TS = P
    NT = (K * N + E * (TS - 1)) // TS
    WE = F + FB + FB * C
    U = 16
    R = 8
    PRE = 2
    BESIDE = 2
    MAGIC = 12582912.0
    BN_EPS = LN_EPS = 1e-5
    ATT_EPS = 1e-6
    col_at, col_n = spans(COLUMNS)
    wide_at, wide_n = spans(WIDE)
    row_at, row_n = spans(ROWS)

    with ExitStack() as ctx:
        def sb(name, shape):
            return ctx.enter_context(nc.sbuf_tensor(name, shape, F32))

        def sem(name):
            return ctx.enter_context(nc.semaphore(name))

        cols_sb = sb("cols_sb", [P, col_n])
        wide_sb = sb("wide_sb", [P, wide_n])
        rows_sb = sb("rows_sb", [1, row_n])
        tokw_sb = sb("tokw_sb", [CTX * D, C])
        w_all = sb("w_all", [P, E, WE])
        w1_sb = sb("w1_sb", [P, SH, F])
        w2_sb = sb("w2_sb", [P, SH, FB, C])
        xt_all = sb("xt_all", [P, B, S])
        store = sb("store", [P, B * C])
        hid_t = store[:, 0:B * S].rearrange("p (b s) -> p b s", b=B)
        x2_all = store[0:S, :].rearrange("p (b c) -> p b c", b=B)
        y_all = sb("y_all", [S, B, C])
        bn_st = sb("bn_st", [P, NCH, 6])
        bn_mv = sb("bn_mv", [P, 2])
        bn_t = sb("bn_t", [P, 4])
        ln_st = sb("ln_st", [S, 2, 6])
        st_all = sb("st_all", [S, B, 6])
        mean1 = sb("mean1", [S, B])
        mean2 = sb("mean2", [S, B])
        half_gap = sb("half_gap", [S, B])
        std1 = sb("std1", [S, B])
        rstd1 = sb("rstd1", [S, B])
        std2 = sb("std2", [S, B])
        rstd2 = sb("rstd2", [S, B])
        shift2 = sb("shift2", [S, B])
        h2 = sb("h2", [S, 2, C])
        xln = sb("xln", [S, 2, C])
        xlnt = sb("xlnt", [P, 2, S])
        w_t = sb("w_t", [P, 4, WE])
        w_flat = w_t[:, :, :].rearrange("p n w -> p (n w)")
        frames = w_flat[0:CTX * D, 0:B * T]
        prob = w_flat[0:S, 0:16 * S].rearrange("s (p h n t) -> s p h n t", p=2, h=2, n=4)
        prob_t = w_flat[0:S, 16 * S:32 * S].rearrange("s (p h n t) -> s p h n t", p=2, h=2, n=4)
        hg_t = sb("hg_t", [P, 4, FB, TS])
        k_t = hg_t[:, :, :, :].rearrange("p n f t -> p (n f t)")[:, 0:4 * G * S].rearrange("p (n g s) -> p n g s", n=4, g=G)
        q_sb = sb("q_sb", [S, 2, H, DH])
        kden = sb("kden", [S, 2, H])
        krec = sb("krec", [S, 2, H])
        pad_q = sb("pad_q", [P, 2 * H * HP])
        qpad = pad_q[0:S, :].rearrange("s (n h d) -> s n h d", n=2, h=H)
        q_t = sb("q_t", [P, 2, G, S])
        pad_v = sb("pad_v", [P, 4 * H * HP])
        v_pad = pad_v[0:S, :].rearrange("s (n h d) -> s n h d", n=4, h=H)
        o_pad = sb("o_pad", [P, 2, G, S])
        bo_v = sb("bo_v", [1, C])
        bo_all = sb("bo_all", [S, C])
        smax = sb("smax", [S, 2, 2, 4])
        orec = sb("orec", [S, 2, H])
        onorm = sb("onorm", [S, 2, H, DH])
        o_t = sb("o_t", [P, 2, S])
        BE = B * E
        pick = w_flat[0:S, 0:K * BE].rearrange("s (k b e) -> s k b e", k=K, b=B)
        logits, left = (w_flat[0:S, (K + n) * BE:(K + n + 1) * BE].rearrange("s (b e) -> s b e", b=B)
                        for n in range(2))
        hits = w_flat[0:S, (K + 1) * BE:(K + 3) * BE].rearrange("s (k b e) -> s k b e", k=2, b=B)
        h_flat = hg_t[:, :, :, :].rearrange("p n f t -> p (n f t)")
        yt = h_flat[:, 0:2 * CW].rearrange("p (n w) -> p n w", n=2)
        chosen = h_flat[0:S, 0:BE].rearrange("s (b e) -> s b e", b=B)
        counts, upto = (h_flat[0:S, n * BE:(n + 1) * BE].rearrange("s (e b) -> s e b", e=E) for n in (1, 2))
        top = sb("top", [S, B, 8])
        place = ctx.enter_context(nc.sbuf_tensor("place", [S, B, 8], mybir.dt.uint32))
        expert_k = sb("expert_k", [S, K, B])
        first = sb("first", [S, B])
        zsum = sb("zsum", [S, B])
        zrec = sb("zrec", [S, B])
        gate_v = sb("gate_v", [S, K, B])
        comb = sb("comb", [S, B, EX])
        comb_b = sb("comb_b", [S, 2, CB, QR])
        comb_t = sb("comb_t", [P, 2, S])
        act_t = sb("act_t", [P, 2, FB, CW])
        total = sb("total", [S, E])
        tiles_of = sb("tiles_of", [S, E])
        tile_pairs = sb("tile_pairs", [S, E, E])
        tile_at = sb("tile_at", [S, E])
        tile_end = sb("tile_end", [S, E])
        slot_at = sb("slot_at", [S, E])
        slot_f = sb("slot_f", [S, K, B])
        slot_tile = sb("slot_tile", [S, K, B])
        slot_row = sb("slot_row", [S, K, B])
        row_bias = slot_row[:, :, :].rearrange("s k b -> s (k b)")
        tile_e = sb("tile_e", [1, NT])
        tile_u = ctx.enter_context(nc.sbuf_tensor("tile_u", [1, NT], mybir.dt.int32))
        item_of, token_of = (w_flat[:, (K + 2) * BE + n * NT:(K + 2) * BE + (n + 1) * NT] for n in range(2))
        item_u = ctx.enter_context(nc.sbuf_tensor("item_u", [P, NT], mybir.dt.uint32))
        token_u = ctx.enter_context(nc.sbuf_tensor("token_u", [P, NT], mybir.dt.uint32))
        b2_sb = h_flat[:, 0:CB * C].rearrange("p (n c) -> p n c", n=CB)
        row_sign = h_flat[0:S, 0:4 * TS].rearrange("s (n r) -> s n r", n=4)
        tile_hot = h_flat[0:S, 4 * TS:4 * TS + 4 * NT].rearrange("s (n t) -> s n t", n=4)
        xg = sb("xg", [P, U, C])
        xg_t = pad_q[:, 0:4 * TS].rearrange("p (n t) -> p n t", n=4)
        yg = pad_v[:, 0:R * C].rearrange("p (n c) -> p n c", n=R)
        shared = x2_all
        back = w_flat[0:S, 0:8 * K * C].rearrange("s (n b k c) -> s n b k c", n=4, b=2, k=K)
        tokens = nc.dram_tensor("tokens", [N, C], F32, kind="Internal").ap()
        results = nc.dram_tensor("results", [1 + K * N + NT * TS, C], F32, kind="Internal").ap()

        ident = wide_sb[:, wide_at["ident"][0]:wide_at["ident"][1]]
        ident_s = ident[0:S, 0:S]
        wk = wide_sb[:, wide_at["wk"][0]:wide_at["wk"][1]].rearrange("p (g c) -> p g c", g=G)
        wqv = wide_sb[:, wide_at["wqv"][0]:wide_at["wqv"][1]]
        wo = wide_sb[:, wide_at["wo"][0]:wide_at["wo"][1]]
        gate_w = wide_sb[:, wide_at["gate"][0]:wide_at["gate"][1]]
        head_of = wide_sb[:, wide_at["head_of"][0]:wide_at["head_of"][1]].rearrange("p (g h) -> p g h", g=G)
        before = wide_sb[0:S, wide_at["before"][0]:wide_at["before"][0] + S]
        every = wide_sb[0:S, wide_at["every"][0]:wide_at["every"][0] + S]
        before_e = wide_sb[0:S, wide_at["before_e"][0]:wide_at["before_e"][1]].rearrange("p (e f) -> p e f", e=E)
        numbers = wide_sb[:, wide_at["numbers"][0]:wide_at["numbers"][1]]
        item_no = wide_sb[0:S, wide_at["item_no"][0]:wide_at["item_no"][1]]
        difference = wide_sb[:, wide_at["difference"][0]:wide_at["difference"][1]]
        spare_no = wide_sb[:, wide_at["spare_no"][0]:wide_at["spare_no"][1]]
        bq = wide_sb[0:S, wide_at["bq"][0]:wide_at["bq"][1]]
        bo = rows_sb[0:1, row_at["bo"][0]:row_at["bo"][1]]
        ones = rows_sb[0:1, row_at["ones"][0]:row_at["ones"][0] + S]

        def column(name, n=0):
            at = col_at[name][0] + n
            return cols_sb[:, at:at + 1]

        ps = ctx.enter_context(nc.psum_tensor("ps", [P, 8, 512], F32))
        PARTS = (slice(0, B - CB), slice(B - CB, B))
        M0, M1 = 6, 7

        LOW, HIGH = (0, 1, 2), (3,)

        frames_in = [sem("frames_in0"), sem("frames_in1")]
        tokw_in = sem("tokw_in")
        params_in = sem("params_in")
        w_in = sem("w_in")
        stored = sem("stored")
        pads_zero = sem("pads_zero")
        relu_ready = sem("relu_ready")
        tok_psum = sem("tok_psum")
        tok_sb = sem("tok_sb")
        tok_stats = sem("tok_stats")
        bn_step = sem("bn_step")
        bn_var = sem("bn_var")
        bn_std = sem("bn_std")
        yt_sb = sem("yt_sb")
        y_psum = sem("y_psum")
        y_sb = sem("y_sb")
        y_stats = sem("y_stats")
        var1 = sem("var1")
        std1_ok = sem("std1_ok")
        rstd1_ok = sem("rstd1_ok")
        ln_step = sem("ln_step")
        ln_sum = sem("ln_sum")
        h2_kept = sem("h2_kept")
        bias_added = sem("bias_added")
        x_ln = sem("x_ln")
        x_t_psum = sem("x_t_psum")
        x_t_sb = sem("x_t_sb")
        k_psum = sem("k_psum")
        k_sb = sem("k_sb")
        qv_psum = sem("qv_psum")
        qv_sb = sem("qv_sb")
        ks_psum = sem("ks_psum")
        ks_read = sem("ks_read")
        ks_rec = sem("ks_rec")
        q_scaled = sem("q_scaled")
        q_t_psum = sem("q_t_psum")
        q_t_sb = sem("q_t_sb")
        s_psum = sem("s_psum")
        s_max = sem("s_max")
        s_sub = sem("s_sub")
        s_exp = sem("s_exp")
        p_t_psum = sem("p_t_psum")
        p_t_sb = sem("p_t_sb")
        bo_psum = sem("bo_psum")
        bo_sb = sem("bo_sb")
        pv_psum = sem("pv_psum")
        o_low = sem("o_low")
        o_high = sem("o_high")
        o_psum = sem("o_psum")
        o_rec = sem("o_rec")
        o_sb = sem("o_sb")
        o_t_psum = sem("o_t_psum")
        o_t_sb = sem("o_t_sb")
        pr_psum = sem("pr_psum")
        h2_sb = sem("h2_sb")
        h2_st = sem("h2_st")
        h2_mv = sem("h2_mv")
        var2 = sem("var2")
        std2_ok = sem("std2_ok")
        rstd2_ok = sem("rstd2_ok")
        x2_sb = sem("x2_sb")
        shift_ok = sem("shift_ok")
        x2_act = sem("x2_act")
        x2t_psum = sem("x2t_psum")
        x2t_sb = sem("x2t_sb")
        lg_psum = sem("lg_psum")
        lg_sb = sem("lg_sb")
        top_sb = sem("top_sb")
        place_sb = sem("place_sb")
        expert_sb = sem("expert_sb")
        pick_sb = sem("pick_sb")
        gates_ok = sem("gates_ok")
        weighed = sem("weighed")
        comb_ok = sem("comb_ok")
        gstep = sem("gstep")
        diff_sb = sem("diff_sb")
        g_diff = sem("g_diff")
        g_exp = sem("g_exp")
        cb_sb = sem("cb_sb")
        b2_zero = sem("b2_zero")
        b2_in = sem("b2_in")
        cbt_psum = sem("cbt_psum")
        cbt_sb = sem("cbt_sb")
        b2_psum = sem("b2_psum")
        b2_added = sem("b2_added")
        chosen_ok = sem("chosen_ok")
        ranks_psum = sem("ranks_psum")
        tokens_out = sem("tokens_out")
        rows_ok = sem("rows_ok")
        sign_sb = sem("sign_sb")
        hot_sb = sem("hot_sb")
        sums_sb = sem("sums_sb")
        found_psum = sem("found_psum")
        items_psum = sem("items_psum")
        items_ok = sem("items_ok")
        tiles_ok = sem("tiles_ok")
        xg_in = [sem(f"xg_in{n}") for n in range(U)]
        w_t_sb = sem("w_t_sb")
        xg_psum = sem("xg_psum")
        xg_sb = sem("xg_sb")
        up_psum = sem("up_psum")
        up_sb = sem("up_sb")
        down_psum = sem("down_psum")
        yg_sb = sem("yg_sb")
        yg_out = [sem(f"yg_out{n}") for n in range(R)]
        back_in = [sem(f"back_in{n}") for n in range(4)]
        part = sem("part")
        routed_added = sem("routed_added")
        y_done = sem("y_done")
        f1_psum = sem("f1_psum")
        f1_sb = sem("f1_sb")
        f2_psum = sem("f2_psum")
        shared_sb = sem("shared_sb")

        def after(eng, s, n, most=B, per=1):
            n = count(n, most)
            if n is not None:
                eng.wait_ge(s, n * per if per != 1 else n)

        def slots(eng, slot):
            lo = 4
            hi = B - 4
            for i in range(-4, lo):
                slot(i, i % 4)
            with eng.Fori(lo, hi - 7, 8) as i:
                for u in range(8):
                    slot(i + u, (lo + u) % 4)
            for i in range(hi, B + 1):
                slot(i, i % 4)

        def lives(b):
            return not isinstance(b, int) or 0 <= b < B

        def pairs(eng, step, lag, lo):
            for i in range(lo):
                step(i, i % 2)
            with eng.Fori(lo, B - 1, 2) as i:
                for u in range(2):
                    step(i + u, u)
            for i in range(B, B + lag):
                step(i, i % 2)

        def items(eng, step):
            for n in range(4):
                step(n, n)
            with eng.Fori(4, K * B - 4 - 19, 20) as n:
                for u in range(20):
                    step(n + u, u % 4)
            for n in range(K * B - 4, K * B):
                step(n, n % 4)

        def slots_of_tiles(eng, slot, between=()):
            cuts = [U, 3 * U, 6 * U, U + (NT - 2 - U) // U * U]
            for i in range(-2, U):
                slot(i, i % U)
            for n in range(len(cuts) - 1):
                with eng.Fori(cuts[n], cuts[n + 1] - (U - 1), U) as i:
                    for u in range(U):
                        slot(i + u, u)
                if between:
                    between[n]()
            for i in range(cuts[-1], NT):
                slot(i, i % U)

        def rounds(t, r, of, first):
            return 16 * (t // of + first) if isinstance(t, int) else t * (16 // of) + (16 * first - 16 // of * r)

        def has(t):
            return not isinstance(t, int) or 0 <= t < NT

        block = ctx.enter_context(nc.Block())

        @block.sync
        def _(sp):
            steps = xT.rearrange("d b t -> d (b t)")
            for lo, hi in ((0, B * T // 2), (B * T // 2, B * T)):
                for i in range(CTX):
                    end = min(hi, B * T - i)
                    sp.dma_start(frames[i * D:(i + 1) * D, lo:end], steps[:, lo + i:end + i])\
                      .then_inc(frames_in[lo // (B * T // 2)], 16)
            sp.dma_start(wide_sb[:, :], wide).then_inc(params_in, 16)
            sp.dma_start(rows_sb[:, :], rows).then_inc(params_in, 16)
            for e in range(0, E, 4):
                sp.dma_start(w_all[:, e:e + 4, 0:F], re_w1[e:e + 4].rearrange("e h f -> h e f")).then_inc(w_in, 16)
                for c in range(FB):
                    sp.dma_start(w_all[:, e:e + 4, F + FB + c * C:F + FB + (c + 1) * C],
                                 re_w2[e:e + 4, c * P:(c + 1) * P].rearrange("e p h -> p e h")).then_inc(w_in, 16)
            sp.dma_start(w_all[:, :, F:F + FB], re_b1).then_inc(w_in, 16)
            sp.dma_start(w1_sb[:, :, :], se_w1.rearrange("e h f -> h e f")).then_inc(w_in, 16)
            sp.dma_start(w2_sb[:, :, :, :].rearrange("p e c h -> p (e c) h"),
                         se_w2.rearrange("e (c p) h -> p (e c) h", p=P)).then_inc(w_in, 16)
            with sp.Fori(0, NCH) as c:
                sp.wait_ge(x2_sb, c * 2 + 2)
                sp.wait_ge(x2_act, c * 2 + 2)
                sp.dma_start(tokens.rearrange("(b s) c -> s b c", s=S)[:, bass.ts(c, CB), :],
                             x2_all[:, bass.ts(c, CB), :]).then_inc(tokens_out, 16)

            sp.wait_ge(b2_zero, 1)
            for s in range(CB):
                sp.dma_start(b2_sb[s * QR:s * QR + E, s, :], re_b2).then_inc(b2_in, 16)
                sp.dma_start(b2_sb[s * QR + E:s * QR + EX, s, :], se_b2).then_inc(b2_in, 16)

            for r in range(R):
                sp.wait_ge(yg_out[r], 16 * ((NT - r + R - 1) // R))
            items_y = results[1:1 + K * N, :].rearrange("(b s k) c -> s b k c", s=S, k=K)

            def fetch(m, r):
                after(sp, routed_added, 2 * m - 6)
                sp.dma_start(back[:, r, :, :, :], items_y[:, bass.ds(2 * m, 2), :, :]).then_inc(back_in[r], 16)

            for m in range(4):
                fetch(m, m)
            with sp.Fori(4, B // 2 - 3, 4) as m:
                for u in range(4):
                    fetch(m + u, u)

            with sp.Fori(0, NCH) as c:
                sp.wait_ge(y_done, c + 1)
                sp.dma_start(out.rearrange("b t c -> t b c")[:, bass.ts(c, CB), :],
                             y_all[:, bass.ts(c, CB), :]).then_inc(stored, 16)
            sp.wait_ge(stored, 16 * NCH)

        W_ALL = 16 * (E // 4 * (1 + FB) + 3)

        @block.gpsimd
        def _(pool):
            nc.gpsimd.memset(qpad[:, :, :, :], 0.0).then_inc(pads_zero, 1)
            nc.gpsimd.memset(v_pad[:, :, :, :], 0.0).then_inc(pads_zero, 1)
            pool.wait_ge(pads_zero, 2)
            nc.gpsimd.memset(v_pad[:, :, :, DH:DH + 1], 1.0).then_inc(pads_zero, 1)
            nc.gpsimd.memset(comb[:, :, :], 1.0 / SH).then_inc(pads_zero, 1)
            nc.gpsimd.memset(comb_b[:, :, :, :], 0.0).then_inc(pads_zero, 1)

            pool.wait_ge(bo_sb, 2)

            def residual(b, p):
                if lives(b):
                    pool.wait_ge(x_ln, b + 1)
                    nc.gpsimd.tensor_tensor(y_all[:, b, :], y_all[:, b, :], bo_all[:, :], ALU.add)\
                      .then_inc(bias_added, 1)
                if lives(b - 5):
                    pool.wait_ge(h2_sb, b - 4)
                    nc.gpsimd.tensor_copy(y_all[:, b - 5, :], h2[:, 1 - p, :]).then_inc(h2_kept, 1)

            pairs(pool, residual, 5, 6)

            pool.wait_ge(rows_ok, 1)
            pool.wait_ge(gates_ok, 1)
            for k in range(K):
                nc.gpsimd.tensor_tensor(pick[:, k, :, :], pick[:, k, :, :],
                                        gate_v[:, k, :].unsqueeze(2).broadcast_to([S, B, E]),
                                        ALU.mult).then_inc(weighed, 1)
            pool.wait_ge(weighed, 2)
            nc.gpsimd.tensor_tensor(comb[:, :, 0:E], pick[:, 0, :, :], pick[:, 1, :, :], ALU.add).then_inc(comb_ok, 1)
            for k in range(2, K):
                pool.wait_ge(weighed, k + 1)
                pool.wait_ge(comb_ok, k - 1)
                nc.gpsimd.tensor_tensor(comb[:, :, 0:E], comb[:, :, 0:E], pick[:, k, :, :],
                                        ALU.add).then_inc(comb_ok, 1)

            pool.wait_ge(tokens_out, 16 * NCH)
            pool.wait_ge(items_ok, 2)

            def load(t):
                if t >= U:
                    pool.wait_ge(xg_psum, t - U + 1)
                pool.indirect_dma_start(xg[:, t % U, :], None, tokens,
                                        bass.IndirectOffsetOnAxis(ap=token_u[:, t:t + 1], axis=0))\
                    .then_inc(xg_in[t % U], 16)

            def save(t):
                pool.wait_ge(yg_sb, t + 1)
                pool.indirect_dma_start(results, bass.IndirectOffsetOnAxis(ap=item_u[:, t:t + 1], axis=0),
                                        yg[:, t % R, :], None).then_inc(yg_out[t % R], 16)

            for t in range(U):
                load(t)
            for t in range(NT):
                save(t)
                if t + U < NT:
                    load(t + U)
            nc.gpsimd.memset(b2_sb[:, :, :], 0.0).then_inc(b2_zero, 1)

        @block.tensor
        def _(pe):
            pe.wait_ge(tokw_in, 32)
            windows = frames.rearrange("p (b t) -> p b t", b=B)

            def tok_chunk(c, p):
                after(pe, tok_sb, c - 1, NCH)
                nc.tensor.matmul(ps[:, p, 0:CW], tokw_sb[:, :], windows[:, c * CB:(c + 1) * CB, 0:S],
                                 start=True, stop=True).then_inc(tok_psum, 1)

            for c in range(NCH):
                if c % (NCH // 2) == 0:
                    pe.wait_ge(frames_in[c // (NCH // 2)], 16 * CTX)
                tok_chunk(c, c % 2)

            pe.wait_ge(params_in, 32)

            for c in range(NCH):
                pe.wait_ge(yt_sb, c + 1)
                after(pe, y_sb, c - 1)
                for s in range(CB):
                    mm = nc.tensor.transpose(ps[0:S, 2 + c % 2, s * C:(s + 1) * C],
                                             yt[:, c % 2, s * S:(s + 1) * S], ident)
                mm.then_inc(y_psum, 1)

            nc.tensor.matmul(ps[0:1, M1, 0:C], column("bv"), wo, start=True, stop=False)
            nc.tensor.matmul(ps[0:1, M1, 0:C], ones[0:1, 0:1], bo, start=False, stop=True).then_inc(bo_psum, 1)
            pe.wait_ge(bo_sb, 1)
            nc.tensor.matmul(ps[0:S, M1, 0:C], ones, bo_v[:, :], start=True, stop=True).then_inc(bo_psum, 1)
            pe.wait_ge(bo_sb, 2)

            def gate(c):
                if c < NCH:
                    pe.wait_ge(x2_sb, (c + 1) * 2)
                    pe.wait_ge(x2_act, (c + 1) * 2)
                    after(pe, x2t_sb, c - 1)
                    for s in range(CB):
                        mm = nc.tensor.transpose(ps[:, c % 2, s * S:(s + 1) * S], x2_all[:, c * CB + s, :], ident_s)
                    mm.then_inc(x2t_psum, 1)
                if c > 0:
                    pe.wait_ge(x2t_sb, c)
                    after(pe, lg_sb, c - 2)
                    for s in range(CB):
                        mm = nc.tensor.matmul(ps[0:S, 3 - c % 2, s * E:(s + 1) * E], xt_all[:, (c - 1) * CB + s, :],
                                              gate_w, start=True, stop=True)
                    mm.then_inc(lg_psum, 1)

            def slot(i, r):
                steady = not isinstance(i, int)

                def m0_free(x, k, q, o):
                    for s, n, per in ((x_t_sb, x, 1), (k_sb, k, G), (q_t_sb, q, 1), (o_t_sb, o, 1)):
                        if n is not None:
                            after(pe, s, n, per=per)

                def m1_free(qv, ks, o, pr):
                    for s, n, per in ((qv_sb, qv, 2), (ks_read, ks, 1), (o_sb, o, 1), (h2_sb, pr, 1)):
                        if n is not None:
                            after(pe, s, n, per=per)

                def scores(half):
                    b = i + 1
                    if not lives(b):
                        return
                    if half == 0:
                        pe.wait_ge(q_t_sb, b + 1)
                    after(pe, s_sub, 2 * b - 1 + half, 2 * B)
                    for j in (2 * half, 2 * half + 1):
                        for g in range(G):
                            rows_j = slice(HP * j, HP * j + HP)
                            mm = nc.tensor.matmul(ps[0:S, j, g * S:(g + 1) * S], q_t[rows_j, (r + 1) % 2, g, :],
                                                  k_t[rows_j, (r + 1) % 4, g, :], start=True, stop=True)
                    mm.then_inc(s_psum, 1)

                def turn_prob(half):
                    b = i
                    if not lives(b):
                        return
                    pe.wait_ge(s_exp, 2 * b + half + 1)
                    after(pe, o_low, b)
                    after(pe, o_high, b)
                    for n in range(4):
                        mm = nc.tensor.transpose(ps[0:S, 4 + half, n * S:(n + 1) * S],
                                                 prob[:, r % 2, half, n, :], ident_s)
                    mm.then_inc(p_t_psum, 1)

                def outputs(g):
                    b = i
                    if not lives(b):
                        return
                    pe.wait_ge(p_t_sb, 2 * b + 2)
                    probs = prob_t[:, r % 2, :, :, :].rearrange("s h (j g) t -> s g (h j) t", g=G)
                    mm = nc.tensor.matmul(ps[:, 4 + g, 0:4 * S],
                                          v_pad[:, r, 4 * g:4 * g + 4, :].rearrange("s h d -> s (h d)"),
                                          probs[:, g, :, :], start=True, stop=True)
                    if g == G - 1:
                        mm.then_inc(pv_psum, 1)

                scores(0)
                if lives(i + 2):
                    b = i + 2
                    after(pe, k_sb, b + 1, per=G)
                    m1_free(*((None, None, None, b - 3) if steady else (b, b, b - 3, b - 3)))
                    nc.tensor.matmul(ps[0:S, M1, 0:2 * C], xlnt[:, r % 2, :], wqv,
                                     start=True, stop=True).then_inc(qv_psum, 1)
                    for g in range(G):
                        mm = nc.tensor.matmul(ps[0:S, M1, 2 * C:2 * C + H], k_t[:, (r + 2) % 4, g, :],
                                              head_of[:, g, :], start=(g == 0), stop=(g == G - 1))
                    mm.then_inc(ks_psum, 1)
                turn_prob(0)
                if lives(i + 3):
                    b = i + 3
                    pe.wait_ge(x_ln, b + 1)
                    m0_free(*((None, None, None, b - 4) if steady else (b, b, b - 1, b - 4)))
                    nc.tensor.transpose(ps[:, M0, 0:S], xln[:, (r + 3) % 2, :], ident_s).then_inc(x_t_psum, 1)
                scores(1)
                turn_prob(1)
                if lives(i - 1):
                    b = i - 1
                    pe.wait_ge(o_low, b + 1)
                    pe.wait_ge(o_high, b + 1)
                    m1_free(*((b + 4, b + 4, None, None) if steady else (b + 4, b + 4, b, b)))
                    for g in range(G):
                        mm = nc.tensor.transpose(ps[0:S, M1, g * P:(g + 1) * P], o_pad[:, (r + 3) % 2, g, :], ident)
                    mm.then_inc(o_psum, 1)
                if not steady and i == B:
                    gate(0)
                if lives(i + 3):
                    b = i + 3
                    pe.wait_ge(x_t_sb, b + 1)
                    m0_free(*((None, None, None, None) if steady else (None, b, b - 1, b - 4)))
                    for g in range(G):
                        mm = nc.tensor.matmul(ps[:, M0, g * S:(g + 1) * S], wk[:, g, :], xlnt[:, (r + 3) % 2, :],
                                              start=True, stop=True)
                    mm.then_inc(k_psum, 1)
                outputs(0)
                if lives(i + 2):
                    b = i + 2
                    pe.wait_ge(q_scaled, b + 1)
                    m0_free(*((None, b + 2, None, None) if steady else (b + 2, b + 2, b, b - 3)))
                    for g in range(G):
                        mm = nc.tensor.transpose(ps[:, M0, g * S:(g + 1) * S],
                                                 qpad[:, r % 2, g * 4:(g + 1) * 4, :].rearrange("s h d -> s (h d)"),
                                                 ident_s)
                    mm.then_inc(q_t_psum, 1)
                if lives(i - 1):
                    b = i - 1
                    pe.wait_ge(o_sb, b + 1)
                    m0_free(*((None, None, None, None) if steady else (b + 5, b + 5, b + 3, b)))
                    nc.tensor.transpose(ps[:, M0, G * S:(G + 1) * S],
                                        onorm[:, (r + 3) % 2, :, :].rearrange("s h d -> s (h d)"),
                                        ident_s).then_inc(o_t_psum, 1)
                if not steady and i == B:
                    gate(1)
                outputs(1)
                if lives(i - 1):
                    b = i - 1
                    pe.wait_ge(o_t_sb, b + 1)
                    m1_free(*((None, None, None, None) if steady else (b + 4, b + 4, b + 1, b)))
                    nc.tensor.matmul(ps[0:S, M1, 0:C], o_t[:, (r + 3) % 2, :], wo,
                                     start=True, stop=True).then_inc(pr_psum, 1)

            slots(pe, slot)

            def up(c, e, fb, banks=FB):
                after(pe, f1_sb, c * (SH * FB) + (e * FB + fb - banks + 1), 10 ** 6)
                nc.tensor.matmul(ps[:, fb % banks, 0:CW], w1_sb[:, e, fb * P:(fb + 1) * P],
                                 xt_all[:, bass.ts(c, CB), :], start=True, stop=True).then_inc(f1_psum, 1)

            def down(c, bank=4):
                for s in range(CB):
                    for e in range(SH):
                        if s == 0:
                            if e == 0:
                                after(pe, shared_sb, c, 10 ** 6)
                            pe.wait_ge(f1_sb, c * (SH * FB) + (e + 1) * FB)
                        for fb in range(FB):
                            mm = nc.tensor.matmul(ps[0:S, bank, s * C:(s + 1) * C], act_t[:, e, fb, s * S:(s + 1) * S],
                                                  w2_sb[:, e, fb, :], start=(e == 0 and fb == 0),
                                                  stop=(e == SH - 1 and fb == FB - 1))
                mm.then_inc(f2_psum, 1)

            def chunk(c, between=None):
                for e in range(SH):
                    for fb in range(FB):
                        up(c, e, fb)
                if between is not None:
                    between()
                down(c)

            for c in range(2, NCH + 1):
                gate(c)
            pe.wait_ge(lg_sb, NCH)

            def ranks():
                pe.wait_ge(chosen_ok, NCH)
                flat = chosen[:, :, :].rearrange("s b e -> s (b e)")
                nc.tensor.matmul(ps[0:S, 7, 0:B * E], every, flat, start=True, stop=True).then_inc(ranks_psum, 1)
                nc.tensor.matmul(ps[0:S, 6, 0:B * E], before, flat, start=True, stop=True).then_inc(ranks_psum, 1)

            pe.wait_ge(w_in, W_ALL)
            for n in range(SH * FB):
                if n == 2:
                    ranks()
                up(0, n // FB, n % FB)
            down(0)
            for n in range(FB):
                up(1, 0, n)

            def item_step(n, p):
                pe.wait_ge(sign_sb, n + 1)
                pe.wait_ge(hot_sb, n + 1)
                start = isinstance(n, int) and n == 0
                stop = isinstance(n, int) and n == K * B - 1
                nc.tensor.matmul(ps[:, 5, 0:NT], row_sign[:, p, :], tile_hot[:, p, :],
                                 start=start, stop=stop).then_inc(items_psum, 1)

            items(pe, item_step)
            pe.wait_ge(sums_sb, 1)
            nc.tensor.matmul(ps[:, 7, 0:NT], difference, item_of[:, :], start=True, stop=True).then_inc(found_psum, 1)
            for n in range(FB):
                up(1, 1, n)
            down(1)

            def slot(i, r):
                if has(i + 2):
                    t, q = i + 2, (r + 2) % U
                    pe.wait_ge(xg_in[q], rounds(t, q, U, 1))
                    after(pe, xg_sb, t - 1, NT)
                    nc.tensor.transpose(ps[:, 6 + q % 2, 0:TS], xg[:, q, :], ident).then_inc(xg_psum, 1)
                if has(i + 1):
                    t, q = i + 1, (r + 1) % U
                    pe.wait_ge(xg_sb, t + 1)
                    pe.wait_ge(w_t_sb, t + 1)
                    if isinstance(t, int) and t == 0:
                        pe.wait_ge(f1_sb, PRE * SH * FB)
                    after(pe, up_sb, (t - 1), NT)
                    for fb in range(FB):
                        mm = nc.tensor.matmul(ps[:, 2 + q % 2, fb * TS:(fb + 1) * TS], w_t[:, q % 4, fb * P:(fb + 1) * P],
                                              xg_t[:, q % 4, :], start=True, stop=True)
                    mm.then_inc(up_psum, 1)
                if has(i):
                    pe.wait_ge(up_sb, i + 1)
                    after(pe, yg_sb, i - 1, NT)
                    for fb in range(FB):
                        at = F + FB + fb * C
                        mm = nc.tensor.matmul(ps[:, 4 + r % 2, 0:C], hg_t[:, r % 4, fb, :], w_t[:, r % 4, at:at + C],
                                              start=(fb == 0), stop=(fb == FB - 1))
                    mm.then_inc(down_psum, 1)

            def first_layer(c):
                after(pe, shared_sb, c)
                for n in range(SH * FB):
                    up(c, n // FB, n % FB, 2)

            slots_of_tiles(pe, slot, (lambda: first_layer(PRE), lambda: down(PRE, 0), lambda: first_layer(PRE + 1)))

            pe.wait_ge(yg_sb, NT)

            def turn_weights(m):
                pe.wait_ge(cb_sb, m + 1)
                after(pe, cbt_sb, m, 10 ** 6)
                for p in range(2):
                    mm = nc.tensor.transpose(ps[:, 5, p * S:(p + 1) * S],
                                             comb_b[:, p, :, :].rearrange("s b e -> s (b e)"), ident_s)
                mm.then_inc(cbt_psum, 1)

            def biases(m):
                pe.wait_ge(cbt_sb, m + 1)
                pe.wait_ge(b2_in, 16 * 2 * CB)
                after(pe, b2_added, 2 * m, 10 ** 6)
                for p in range(2):
                    nc.tensor.matmul(ps[0:S, 6 + p, 0:CB * C], comb_t[:, p, :],
                                     b2_sb[:, :, :].rearrange("p n c -> p (n c)"),
                                     start=True, stop=True).then_inc(b2_psum, 1)

            def last_chunk(m):
                turn_weights(m)
                chunk(m + (PRE + BESIDE), lambda: biases(m))

            down(PRE + BESIDE - 1)
            last_chunk(0)
            with pe.Fori(1, NCH // 2) as m:
                last_chunk(m)

        @block.scalar
        def _(act):
            act.dma_start(tokw_sb[:, :], tok_w).then_inc(tokw_in, 16)
            act.dma_start(cols_sb[:, :], columns).then_inc(tokw_in, 16)
            act.wait_ge(tokw_in, 32)
            nc.scalar.activation(bn_t[:, 0:1], column("tok_b"), ACT.Relu).then_inc(relu_ready, 1)
            for c in range(NCH):
                act.wait_ge(tok_psum, c + 1)
                nc.scalar.activation(hid_t[:, c * CB:(c + 1) * CB, :].rearrange("p b s -> p (b s)"),
                                     ps[:, c % 2, 0:CW], ACT.Relu, bias=column("tok_b")).then_inc(tok_sb, 1)
            act.wait_ge(bn_var, 1)
            nc.scalar.activation(bn_t[:, 1:2], bn_t[:, 0:1], ACT.Sqrt).then_inc(bn_std, 1)

            act.wait_ge(bn_step, 5)
            for c in range(NCH + 1):
                if c < NCH:
                    after(act, y_psum, c - 1)
                    nc.scalar.activation(yt[:, c % 2, :], hid_t[:, c * CB:(c + 1) * CB, :].rearrange("p b s -> p (b s)"),
                                         ACT.Identity, scale=bn_t[:, 2:3], bias=bn_t[:, 3:4]).then_inc(yt_sb, 1)
                if c > 0:
                    act.wait_ge(y_psum, c)
                    nc.scalar.copy(y_all[:, (c - 1) * CB:c * CB, :].rearrange("s b c -> s (b c)"),
                                   ps[0:S, 3 - c % 2, 0:CB * C]).then_inc(y_sb, 1)

            act.wait_ge(var1, 1)
            nc.scalar.activation(std1[:, :], rstd1[:, :], ACT.Sqrt).then_inc(std1_ok, 1)
            act.wait_ge(params_in, 32)
            act.wait_ge(bo_psum, 1)
            nc.scalar.copy(bo_v[:, :], ps[0:1, M1, 0:C]).then_inc(bo_sb, 1)
            act.wait_ge(bo_psum, 2)
            nc.scalar.copy(bo_all[:, :], ps[0:S, M1, 0:C]).then_inc(bo_sb, 1)

            def deviation(part):
                act.wait_ge(var2, part + 1)
                nc.scalar.activation(std2[:, PARTS[part]], rstd2[:, PARTS[part]], ACT.Sqrt).then_inc(std2_ok, 1)

            def gate(c):
                if c < NCH:
                    act.wait_ge(shift_ok, 2 if c == NCH - 1 else 1)
                    for b in range(c * CB + 2, (c + 1) * CB):
                        nc.scalar.activation(x2_all[:, b, :], y_all[:, b, :], ACT.Identity, scale=rstd2[:, b:b + 1],
                                             bias=shift2[:, b:b + 1]).then_inc(x2_act, 1)
                if c > 0:
                    act.wait_ge(x2t_psum, c)
                    nc.scalar.copy(xt_all[:, (c - 1) * CB:c * CB, :].rearrange("p b s -> p (b s)"),
                                   ps[:, 1 - c % 2, 0:CW]).then_inc(x2t_sb, 1)

            def slot(i, r):
                last = isinstance(i, int) and i >= B - 1

                def exp(half):
                    b = i + 1
                    if lives(b):
                        act.wait_ge(s_sub, 2 * b + half + 1)
                        x = prob[:, (r + 1) % 2, half, :, :]
                        nc.scalar.activation(x, x, ACT.Exp).then_inc(s_exp, 1)

                def keep_prob_t(half):
                    b = i
                    if lives(b):
                        act.wait_ge(p_t_psum, 2 * b + half + 1)
                        after(act, pv_psum, b - 1)
                        nc.scalar.copy(prob_t[:, r % 2, half, :, :].rearrange("s n t -> s (n t)"),
                                       ps[0:S, 4 + half, 0:4 * S]).then_inc(p_t_sb, 1)

                keep_prob_t(0)
                if lives(i + 3):
                    b = i + 3
                    act.wait_ge(x_t_psum, b + 1)
                    after(act, qv_psum, b - 1)
                    nc.scalar.copy(xlnt[:, (r + 3) % 2, :], ps[:, M0, 0:S]).then_inc(x_t_sb, 1)
                exp(0)
                keep_prob_t(1)
                if lives(i + 3):
                    b = i + 3
                    act.wait_ge(k_psum, b + 1)
                    after(act, s_psum, 2 * b - 6, 2 * B)
                    for g in range(G):
                        nc.scalar.activation(k_t[:, (r + 3) % 4, g, :], ps[:, M0, g * S:(g + 1) * S], ACT.Relu,
                                             bias=column("bk", g)).then_inc(k_sb, 1)
                if lives(i + 2):
                    b = i + 2
                    act.wait_ge(q_t_psum, b + 1)
                    after(act, o_t_psum, b - 2)
                    after(act, s_psum, 2 * b - 2, 2 * B)
                    nc.scalar.copy(q_t[:, r % 2, :, :].rearrange("p g s -> p (g s)"),
                                   ps[:, M0, 0:G * S]).then_inc(q_t_sb, 1)
                if last and i == B:
                    gate(0)
                if lives(i - 1):
                    b = i - 1
                    act.wait_ge(o_t_psum, b + 1)
                    after(act, pr_psum, b - 1)
                    nc.scalar.copy(o_t[:, (r + 3) % 2, :], ps[:, M0, G * S:(G + 1) * S]).then_inc(o_t_sb, 1)
                exp(1)
                if last and i == B - 1:
                    deviation(0)
                if last and i == B:
                    gate(1)
                if lives(i):
                    b = i
                    act.wait_ge(pv_psum, b + 1)
                    after(act, o_psum, b - 1)
                    for j in LOW:
                        rows_j = slice(HP * j, HP * j + HP)
                        cp = nc.scalar.copy(o_pad[rows_j, r % 2, :, :], ps[rows_j, 4:6, j * S:(j + 1) * S])
                    cp.then_inc(o_low, 1)

            slots(act, slot)
            gate(2)
            gate(3)
            deviation(1)
            for c in range(4, NCH + 1):
                gate(c)

            def gelu(c, e, fb, banks=FB):
                act.wait_ge(f1_psum, c * (SH * FB) + (e * FB + fb + 1))
                nc.scalar.activation(act_t[:, e, fb, :], ps[:, fb % banks, 0:CW], ACT.Gelu,
                                     bias=column("b1", e * FB + fb)).then_inc(f1_sb, 1)

            act.wait_ge(g_diff, NCH)
            nc.scalar.activation(left[:, :, :], left[:, :, :], ACT.Exp).then_inc(g_exp, 1)
            nc.scalar.activation(gate_v[:, :, :], gate_v[:, :, :], ACT.Exp).then_inc(g_exp, 1)

            act.wait_ge(g_diff, NCH + 1)
            nc.scalar.activation(gate_v[:, :, :], gate_v[:, :, :], ACT.Exp).then_inc(g_exp, 1)

            def mean(c, bank=4):
                act.wait_ge(f2_psum, c + 1)
                nc.scalar.activation(shared[:, bass.ts(c, CB), :].rearrange("s b c -> s (b c)"),
                                     ps[0:S, bank, 0:CB * C], ACT.Copy, scale=1.0 / SH).then_inc(shared_sb, 1)

            def chunk(c):
                after(act, f2_psum, c, 10 ** 6)
                for e in range(SH):
                    for fb in range(FB):
                        gelu(c, e, fb)
                mean(c)

            act.wait_ge(tokens_out, 16 * NCH)
            for n in range(SH * FB):
                gelu(0, n // FB, n % FB)
            mean(0)
            for n in range(FB):
                gelu(1, 0, n)

            def item_step(n, p):
                act.wait_ge(rows_ok, 1)
                after(act, items_psum, n - 3, K * B)
                nc.scalar.activation(row_sign[:, p, :], numbers[0:S, 0:TS], ACT.Sign,
                                     bias=row_bias[:, bass.ds(n, 1)]).then_inc(sign_sb, 1)

            items(act, item_step)
            for n in range(FB):
                gelu(1, 1, n)
            mean(1)

            def slot(i, r):
                if has(i + 1):
                    t, q = i + 1, (r + 1) % U
                    act.wait_ge(up_psum, t + 1)
                    after(act, down_psum, t - 3, NT)
                    for fb in range(FB):
                        g = nc.scalar.activation(hg_t[:, q % 4, fb, :], ps[:, 2 + q % 2, fb * TS:(fb + 1) * TS], ACT.Gelu,
                                                 bias=w_t[:, q % 4, F + fb:F + fb + 1])
                    g.then_inc(up_sb, 1)

            def gelus(c):
                for n in range(SH * FB):
                    gelu(c, n // FB, n % FB, 2)

            slots_of_tiles(act, slot, (lambda: gelus(PRE), lambda: mean(PRE, 0), lambda: gelus(PRE + 1)))

            def last_chunk(m):
                act.wait_ge(cbt_psum, m + 1)
                after(act, b2_psum, 2 * m, 10 ** 6)
                nc.scalar.copy(comb_t[:, :, :].rearrange("p n s -> p (n s)"), ps[:, 5, 0:2 * S]).then_inc(cbt_sb, 1)
                chunk(m + (PRE + BESIDE))

            mean(PRE + BESIDE - 1)
            last_chunk(0)
            with act.Fori(1, NCH // 2) as m:
                last_chunk(m)

        @block.vector
        def _(dve):
            v = nc.vector
            dve.wait_ge(tokw_in, 32)
            for c in range(NCH):
                dve.wait_ge(tok_sb, c + 1)
                v.bn_stats(bn_st[:, c, :], hid_t[:, c * CB:(c + 1) * CB, :].rearrange("p b s -> p (b s)"))\
                 .then_inc(tok_stats, 1)
            dve.wait_ge(tok_stats, NCH)
            v.bn_aggr(bn_mv[:, :], bn_st[:, :, :]).then_inc(bn_step, 1)
            dve.wait_ge(bn_step, 1)
            dve.wait_ge(relu_ready, 1)
            v.tensor_scalar(bn_t[:, 0:1], bn_mv[:, 1:2], BN_EPS, None, ALU.add).then_inc(bn_var, 1)
            dve.wait_ge(bn_std, 1)
            v.reciprocal(bn_t[:, 2:3], bn_t[:, 1:2]).then_inc(bn_step, 1)
            dve.wait_ge(bn_step, 2)
            v.tensor_tensor(bn_t[:, 2:3], bn_t[:, 2:3], column("tok_gamma"), ALU.mult).then_inc(bn_step, 1)
            dve.wait_ge(bn_step, 3)
            v.scalar_tensor_tensor(bn_t[:, 3:4], bn_mv[:, 0:1], bn_t[:, 2:3], column("tok_beta"),
                                   ALU.mult, ALU.subtract).then_inc(bn_step, 1)
            dve.wait_ge(bn_step, 4)
            v.tensor_scalar(bn_t[:, 3:4], bn_t[:, 3:4], -1.0, None, ALU.mult).then_inc(bn_step, 1)

            def join_stats(mean, var, of, done, ready):
                v.tensor_tensor(mean[:, of], st_all[:, of, 1], st_all[:, of, 4], ALU.add).then_inc(ln_step, 1)
                v.tensor_tensor(half_gap[:, of], st_all[:, of, 1], st_all[:, of, 4], ALU.subtract).then_inc(ln_step, 1)
                dve.wait_ge(ln_step, done + 2)
                v.tensor_scalar(mean[:, of], mean[:, of], 0.5, None, ALU.mult).then_inc(ln_step, 1)
                v.scalar_tensor_tensor(half_gap[:, of], half_gap[:, of], 0.25 * C, half_gap[:, of],
                                       ALU.mult, ALU.mult).then_inc(ln_step, 1)
                dve.wait_ge(ln_step, done + 4)
                v.tensor_tensor(var[:, of], st_all[:, of, 2], st_all[:, of, 5], ALU.add).then_inc(ln_sum, 1)
                dve.wait_ge(ln_sum, done // 2 + 1)
                v.tensor_tensor(var[:, of], var[:, of], half_gap[:, of], ALU.add).then_inc(ln_sum, 1)
                dve.wait_ge(ln_sum, done // 2 + 2)
                v.tensor_scalar(var[:, of], var[:, of], 1.0 / C, LN_EPS, ALU.mult, ALU.add).then_inc(ready, 1)

            for b in range(B):
                dve.wait_ge(y_sb, b // CB + 1)
                v.bn_stats(st_all[:, b, :], y_all[:, b, :]).then_inc(y_stats, 1)
            dve.wait_ge(y_stats, B)
            join_stats(mean1, rstd1, slice(0, B), 0, var1)
            dve.wait_ge(std1_ok, 1)
            v.reciprocal(rstd1[:, :], std1[:, :]).then_inc(rstd1_ok, 1)
            dve.wait_ge(rstd1_ok, 1)
            dve.wait_ge(pads_zero, 5)

            steps = [0]

            def then(ins):
                steps[0] += 1
                ins.then_inc(gstep, 1)
                dve.wait_ge(gstep, steps[0])

            def sequences(c):
                return slice(c * CB, (c + 1) * CB)

            def variance(part):
                done = PARTS[part].stop
                dve.wait_ge(h2_mv, done)
                join_stats(mean2, rstd2, PARTS[part], 4 + 4 * part, var2)

            def scale(part):
                of = PARTS[part]
                dve.wait_ge(std2_ok, part + 1)
                v.reciprocal(rstd2[:, of], std2[:, of]).then_inc(rstd2_ok, 1)
                dve.wait_ge(rstd2_ok, part + 1)
                v.scalar_tensor_tensor(shift2[:, of], mean2[:, of], -1.0, rstd2[:, of], ALU.mult, ALU.mult)\
                 .then_inc(shift_ok, 1)
                dve.wait_ge(h2_kept, of.stop)

            def gate(c):
                x, lg, pk = c, c - 3, c - 4

                def normalise(of):
                    dve.wait_ge(shift_ok, 2 if x == NCH - 1 else 1)
                    for b in of:
                        v.tensor_scalar(x2_all[:, b, :], y_all[:, b, :], mean2[:, b:b + 1], rstd2[:, b:b + 1],
                                        ALU.subtract, ALU.mult).then_inc(x2_sb, 1)

                if 0 <= lg < NCH:
                    dve.wait_ge(lg_psum, lg + 1)
                    v.tensor_copy(logits[:, sequences(lg), :].rearrange("s b e -> s (b e)"),
                                  ps[0:S, 2 + lg % 2, 0:CB * E]).then_inc(lg_sb, 1)
                if 0 <= pk < NCH:
                    dve.wait_ge(place_sb, CB * (pk + 1))
                    v.tensor_copy(expert_k[:, :, sequences(pk)],
                                  place[:, sequences(pk), 0:K].rearrange("s b k -> s k b")).then_inc(expert_sb, 1)
                if x < NCH:
                    normalise(range(x * CB, x * CB + 1))
                if 0 <= lg < NCH:
                    dve.wait_ge(lg_sb, lg + 1)
                    for b in range(lg * CB, (lg + 1) * CB):
                        v.max(out=top[:, b, :], in_=logits[:, b, :]).then_inc(top_sb, 1)
                if 0 <= pk < NCH:
                    dve.wait_ge(expert_sb, pk + 1)
                    v.tensor_tensor(pick[:, :, sequences(pk), :],
                                    expert_k[:, :, sequences(pk)].unsqueeze(3).broadcast_to([S, K, CB, E]),
                                    numbers[0:S, 0:E].unsqueeze(1).unsqueeze(1).broadcast_to([S, K, CB, E]),
                                    ALU.is_equal).then_inc(pick_sb, 1)
                if x < NCH:
                    normalise(range(x * CB + 1, x * CB + 2))
                if 0 <= lg < NCH:
                    for b in range(lg * CB, (lg + 1) * CB):
                        dve.wait_ge(top_sb, b + 1)
                        v.max_index(out=place[:, b, :], in_max=top[:, b, :], in_values=logits[:, b, :])\
                         .then_inc(place_sb, 1)
                if 0 <= pk < NCH:
                    dve.wait_ge(pick_sb, pk + 1)
                    v.tensor_reduce(chosen[:, sequences(pk), :],
                                    pick[:, :, sequences(pk), :].rearrange("s k b e -> s b e k"),
                                    AX.X, ALU.add).then_inc(chosen_ok, 1)
                if 0 <= lg < NCH:
                    v.tensor_tensor(left[:, sequences(lg), :], logits[:, sequences(lg), :],
                                    top[:, sequences(lg), 0:1].broadcast_to([S, CB, E]), ALU.subtract)\
                     .then_inc(diff_sb, 1)
                    v.tensor_tensor(gate_v[:, :, sequences(lg)],
                                    top[:, sequences(lg), 0:K].rearrange("s b k -> s k b"),
                                    top[:, sequences(lg), 0:1].rearrange("s b k -> s k b")
                                    .broadcast_to([S, K, CB]), ALU.subtract).then_inc(g_diff, 1)

            def slot(i, r):
                last = isinstance(i, int) and i == B
                if last:
                    scale(0)
                    gate(0)
                scored, summed, normed = lives(i + 1), lives(i + 2), lives(i - 1)
                x = prob[:, (r + 1) % 2, :, :, :].rearrange("s h (j g) t -> s h j g t", g=G)

                def row_max(half):
                    scores = ps[0:S, 2 * half:2 * half + 2, 0:G * S].rearrange("s j (g t) -> s j g t", g=G)
                    return scores, smax[:, (r + 1) % 2, half, :].rearrange("s (j g) -> s j g", g=G)

                def find_max(half):
                    if scored:
                        dve.wait_ge(s_psum, 2 * (i + 1) + half + 1)
                        scores, top4 = row_max(half)
                        v.tensor_reduce(top4, scores, AX.X, ALU.max).then_inc(s_max, 1)

                def below_max(half):
                    if scored:
                        scores, top4 = row_max(half)
                        dve.wait_ge(s_max, 2 * (i + 1) + half + 1)
                        after(dve, p_t_psum, 2 * (i + 1) - 3 + half, 2 * B)
                        v.tensor_tensor(x[:, half, :, :, :], scores,
                                        top4.unsqueeze(3).broadcast_to([S, 2, G, S]), ALU.subtract).then_inc(s_sub, 1)

                find_max(0)
                below_max(0)
                if summed:
                    b = i + 2
                    dve.wait_ge(qv_psum, b + 1)
                    dve.wait_ge(ks_psum, b + 1)
                    v.tensor_scalar(kden[:, r % 2, :], ps[0:S, M1, 2 * C:2 * C + H], ATT_EPS, None,
                                    ALU.add).then_inc(ks_read, 1)
                    after(dve, q_scaled, b - 1)
                    v.tensor_tensor(q_sb[:, r % 2, :, :].rearrange("s h d -> s (h d)"), ps[0:S, M1, 0:C], bq,
                                    ALU.add).then_inc(qv_sb, 1)
                    dve.wait_ge(ks_read, b + 1)
                    v.reciprocal(krec[:, r % 2, :], kden[:, r % 2, :]).then_inc(ks_rec, 1)
                    after(dve, pv_psum, b - 3)
                    v.tensor_copy(v_pad[:, (r + 2) % 4, :, 0:DH],
                                  ps[0:S, M1, C:2 * C].rearrange("s (h d) -> s h d", d=DH)).then_inc(qv_sb, 1)
                    dve.wait_ge(ks_rec, b + 1)
                    dve.wait_ge(qv_sb, 2 * b + 1)
                    after(dve, q_t_psum, b - 1)
                    v.scalar_tensor_tensor(qpad[:, r % 2, :, 0:DH], q_sb[:, r % 2, :, :], 0.0,
                                           krec[:, r % 2, :].unsqueeze(2).broadcast_to([S, H, DH]),
                                           ALU.max, ALU.mult).then_inc(q_scaled, 1)
                find_max(1)
                if normed:
                    b = i - 1
                    dve.wait_ge(o_psum, b + 1)
                    o = ps[0:S, M1, 0:H * HP].rearrange("s (h d) -> s h d", d=HP)
                    v.reciprocal(orec[:, (r + 3) % 2, :], o[:, :, DH]).then_inc(o_rec, 1)
                    dve.wait_ge(o_rec, b + 1)
                    after(dve, o_t_psum, b - 1)
                    v.tensor_tensor(onorm[:, (r + 3) % 2, :, :], o[:, :, 0:DH],
                                    orec[:, (r + 3) % 2, :].unsqueeze(2).broadcast_to([S, H, DH]),
                                    ALU.mult).then_inc(o_sb, 1)
                if last:
                    gate(1)
                below_max(1)
                if lives(i + 4):
                    b = i + 4
                    after(dve, x_t_psum, b - 1)
                    v.tensor_scalar(xln[:, r % 2, :], y_all[:, b, :], mean1[:, bass.ds(b, 1)],
                                    rstd1[:, bass.ds(b, 1)], ALU.subtract, ALU.mult).then_inc(x_ln, 1)
                if lives(i):
                    b = i
                    dve.wait_ge(pv_psum, b + 1)
                    after(dve, o_psum, b - 1)
                    for j in HIGH:
                        rows_j = slice(HP * j, HP * j + HP)
                        cp = v.tensor_copy(o_pad[rows_j, r % 2, :, :], ps[rows_j, 4:6, j * S:(j + 1) * S])
                    cp.then_inc(o_high, 1)
                if normed:
                    b = i - 1
                    dve.wait_ge(pr_psum, b + 1)
                    dve.wait_ge(bias_added, b + 1)
                    after(dve, h2_kept, b - 1)
                    v.tensor_tensor(h2[:, (r + 3) % 2, :], ps[0:S, M1, 0:C], y_all[:, b, :],
                                    ALU.add).then_inc(h2_sb, 1)
                    dve.wait_ge(h2_sb, b + 1)
                    v.bn_stats(ln_st[:, (r + 3) % 2, :], h2[:, (r + 3) % 2, :]).then_inc(h2_st, 1)
                    dve.wait_ge(h2_st, b + 1)
                    v.tensor_copy(st_all[:, b, :], ln_st[:, (r + 3) % 2, :]).then_inc(h2_mv, 1)
                if isinstance(i, int) and i == B - 2:
                    variance(0)

            slots(dve, slot)
            gate(2)
            variance(1)
            gate(3)
            gate(4)
            scale(1)
            for c in range(5, NCH + 4):
                gate(c)

            over_picked = [S, K, B]
            dve.wait_ge(g_exp, 2)
            then(v.tensor_reduce(zsum[:, :], left[:, :, :], AX.X, ALU.add))
            then(v.reciprocal(zrec[:, :], zsum[:, :]))
            then(v.tensor_tensor(gate_v[:, :, :], gate_v[:, :, :], zrec[:, :].unsqueeze(1).broadcast_to(over_picked),
                                 ALU.mult))
            then(v.tensor_copy(first[:, :], gate_v[:, 0, :]))
            v.tensor_tensor(gate_v[:, :, :], gate_v[:, :, :], first[:, :].unsqueeze(1).broadcast_to(over_picked),
                            ALU.subtract).then_inc(g_diff, 1)
            dve.wait_ge(g_exp, 3)
            then(v.tensor_reduce(zsum[:, :], gate_v[:, :, :].rearrange("s k b -> s b k"), AX.X, ALU.add))
            then(v.reciprocal(zrec[:, :], zsum[:, :]))
            v.tensor_tensor(gate_v[:, :, :], gate_v[:, :, :], zrec[:, :].unsqueeze(1).broadcast_to(over_picked),
                            ALU.mult).then_inc(gates_ok, 1)

            dve.wait_ge(ranks_psum, 2)
            cnt = ps[0:S, 7, 0:B * E].rearrange("s (b e) -> s e b", e=E)
            rank_in = ps[0:S, 6, 0:B * E].rearrange("s (b e) -> s e b", e=E)
            then(v.tensor_copy(counts[:, :, :], cnt))
            flat = counts[:, :, :].rearrange("s e b -> s (e b)")
            then(v.tensor_tensor_scan(upto[:, :, :].rearrange("s e b -> s (e b)"), flat, flat, 0.0, ALU.add, ALU.max))
            then(v.tensor_copy(total[:, 0:1], upto[:, 0, B - 1:B]))
            then(v.tensor_tensor(total[:, 1:E], upto[:, 1:E, B - 1], upto[:, 0:E - 1, B - 1], ALU.subtract))
            then(v.tensor_scalar(tiles_of[:, :], total[:, :], 1.0 / TS, (TS - 1) / (2.0 * TS), ALU.mult, ALU.add))
            then(v.tensor_scalar(tiles_of[:, :], tiles_of[:, :], MAGIC, None, ALU.add))
            then(v.tensor_scalar(tiles_of[:, :], tiles_of[:, :], MAGIC, None, ALU.subtract))
            then(v.tensor_tensor(tile_pairs[:, :, :], before_e, tiles_of[:, :].unsqueeze(1).broadcast_to([S, E, E]),
                                 ALU.mult))
            then(v.tensor_reduce(tile_at[:, :], tile_pairs[:, :, :], AX.X, ALU.add))
            then(v.tensor_tensor(tile_end[:, :], tile_at[:, :], tiles_of[:, :], ALU.add))
            then(v.tensor_scalar(slot_at[:, :], tile_at[:, :], float(TS), None, ALU.mult))
            then(v.tensor_tensor(slot_at[:, 1:E], slot_at[:, 1:E], upto[:, 0:E - 1, B - 1], ALU.subtract))
            then(v.tensor_tensor(upto[:, :, :], upto[:, :, :], rank_in, ALU.add))
            then(v.tensor_tensor(upto[:, :, :], upto[:, :, :],
                                 slot_at[:, :].unsqueeze(2).broadcast_to([S, E, B]), ALU.add))
            for k in range(0, K, 2):
                then(v.tensor_tensor(hits[:, :, :, :], pick[:, k:k + 2, :, :],
                                     upto[:, :, :].rearrange("s e b -> s b e").unsqueeze(1)
                                     .broadcast_to([S, 2, B, E]), ALU.mult))
                then(v.tensor_reduce(slot_f[:, k:k + 2, :], hits[:, :, :, :], AX.X, ALU.add))
            then(v.tensor_scalar(slot_tile[:, :, :], slot_f[:, :, :], 1.0 / TS, -(TS - 1) / (2.0 * TS),
                                 ALU.mult, ALU.add))
            then(v.tensor_scalar(slot_tile[:, :, :], slot_tile[:, :, :], MAGIC, None, ALU.add))
            then(v.tensor_scalar(slot_tile[:, :, :], slot_tile[:, :, :], MAGIC, None, ALU.subtract))
            then(v.scalar_tensor_tensor(slot_row[:, :, :], slot_tile[:, :, :], float(TS), slot_f[:, :, :],
                                        ALU.mult, ALU.subtract))
            v.tensor_scalar(slot_row[:, :, :], slot_row[:, :, :], 0.5, None, ALU.add).then_inc(rows_ok, 1)
            tile_at_n = slot_tile[:, :, :].rearrange("s k b -> s (k b)")

            def item_step(n, p):
                after(dve, items_psum, n - 3, K * B)
                v.tensor_scalar(tile_hot[:, p, :], numbers[0:S, 0:NT], tile_at_n[:, bass.ds(n, 1)],
                                item_no[:, bass.ds(n, 1)], ALU.is_equal, ALU.mult).then_inc(hot_sb, 1)

            items(dve, item_step)
            dve.wait_ge(items_psum, K * B)
            v.tensor_copy(item_of[:, :], ps[:, 5, 0:NT]).then_inc(sums_sb, 1)
            dve.wait_ge(found_psum, 1)
            found = ps[:, 7, 0:NT]
            then(v.scalar_tensor_tensor(item_of[:, :], found, 0.0, spare_no, ALU.is_equal, ALU.mult))
            then(v.tensor_scalar(token_of[:, :], found, 1.0 / K, -(K + 1) / (2.0 * K), ALU.mult, ALU.add))
            then(v.tensor_tensor(item_of[:, :], item_of[:, :], found, ALU.add))
            then(v.tensor_scalar(token_of[:, :], token_of[:, :], MAGIC, None, ALU.add))
            then(v.tensor_scalar(token_of[:, :], token_of[:, :], MAGIC, 0.0, ALU.subtract, ALU.max))
            v.tensor_copy(token_u[:, :], token_of[:, :]).then_inc(items_ok, 1)
            v.tensor_copy(item_u[:, :], item_of[:, :]).then_inc(items_ok, 1)
            ended = h_flat[0:1, 0:NT * (E - 1)].rearrange("o (t e) -> o t e", t=NT)
            then(v.tensor_tensor(ended, tile_end[0:1, 0:E - 1].unsqueeze(1).broadcast_to([1, NT, E - 1]),
                                 numbers[0:1, 0:NT].unsqueeze(2).broadcast_to([1, NT, E - 1]), ALU.is_le))
            then(v.tensor_reduce(tile_e[:, :], ended, AX.X, ALU.add))
            v.tensor_copy(tile_u[:, :], tile_e[:, :]).then_inc(tiles_ok, 1)
            dve.wait_ge(tiles_ok, 1)
            dve.wait_ge(comb_ok, K - 1)
            dve.wait_ge(gates_ok, 1)

            def weights(t, r):
                e = dve.value_load(tile_u[0:1, bass.ds(t, 1)], min_val=0, max_val=E - 1)
                after(dve, down_psum, t - 3, NT)
                v.tensor_copy(w_t[:, r % 4, :], w_all[:, e, :]).then_inc(w_t_sb, 1)

            weights(0, 0)

            def slot(i, r):
                if has(i + 2):
                    t, q = i + 2, (r + 2) % U
                    dve.wait_ge(xg_psum, t + 1)
                    after(dve, up_psum, t - 3, NT)
                    v.tensor_copy(xg_t[:, q % 4, :], ps[:, 6 + q % 2, 0:TS]).then_inc(xg_sb, 1)
                if has(i + 3):
                    weights(i + 3, r + 3)
                if has(i):
                    dve.wait_ge(down_psum, i + 1)
                    if not (isinstance(i, int) and i < R):
                        dve.wait_ge(yg_out[r % R], rounds(i, r % R, R, 0))
                    v.tensor_copy(yg[:, r % R, :], ps[:, 4 + r % 2, 0:C]).then_inc(yg_sb, 1)

            slots_of_tiles(dve, slot)

            def combine(b, r, half):
                for k in range(K):
                    ins = v.scalar_tensor_tensor(y_all[:, b, :], back[:, r, half, k, :], gate_v[:, k, bass.ds(b, 1)],
                                                 y_all[:, b, :], ALU.mult, ALU.add)
                    if k < K - 1:
                        ins.then_inc(part, 1)
                        dve.wait_ge(part, b * (K - 1) + (k + 1))
                    else:
                        ins.then_inc(routed_added, 1)

            def turn_in(m):
                after(dve, cbt_psum, m, 10 ** 6)
                for p in range(2):
                    cp = v.tensor_copy(comb_b[:, p, :, 0:EX], comb[:, bass.ds(8 * m + CB * p, CB), :])
                cp.then_inc(cb_sb, 1)

            def part_of_tail(m, last):
                if not last:
                    turn_in(m + 1)
                for u in range(8):
                    if u % 2 == 0:
                        dve.wait_ge(back_in[u // 2], 16 * m + 16)
                    combine(8 * m + u, u // 2, u % 2)
                dve.wait_ge(routed_added, 8 * m + 8)
                for p in range(2):
                    dve.wait_ge(b2_psum, 2 * m + p + 1)
                    seqs = y_all[:, bass.ds(8 * m + CB * p, CB), :].rearrange("s b c -> s (b c)")
                    v.tensor_tensor(seqs, ps[0:S, 6 + p, 0:CB * C], seqs, ALU.add).then_inc(b2_added, 1)
                for p in range(2):
                    dve.wait_ge(shared_sb, 2 * m + p + 1)
                    dve.wait_ge(b2_added, 2 * m + p + 1)
                    seqs = bass.ds(8 * m + CB * p, CB)
                    v.tensor_tensor(y_all[:, seqs, :], y_all[:, seqs, :], shared[:, seqs, :],
                                    ALU.add).then_inc(y_done, 1)

            turn_in(0)
            part_of_tail(0, False)
            with dve.Fori(1, B // 8 - 1) as m:
                part_of_tail(m, False)
            part_of_tail(B // 8 - 1, True)


def kernel(**inputs):
    import numpy as np
    import concourse.bacc as bacc
    from concourse import mybir as mb
    from concourse.bass_utils import run_bass_kernel_spmd

    a = {k: np.asarray(v) for k, v in inputs.items()}
    H, DH = 8, 16
    C = a["L0_tok_W"].shape[0]
    E, _, F = a["L0_ffn_re_w1"].shape
    B, T, D = a["x"].shape
    f32 = np.float32

    def padded_heads(w):
        o = np.zeros(w.shape[:-1] + (H, 2 * DH), f32)
        o[..., :DH] = w.reshape(w.shape[:-1] + (H, DH))
        return o.reshape(w.shape[:-1] + (2 * H * DH,))

    S, K = T - a["L0_tok_W"].shape[1] // D + 1, 4
    NT = (K * B * S + E * (P - 1)) // P
    item_no = np.zeros((P, K, B), f32)
    item_no[0:S] = 1 + (np.arange(B)[None, None, :] * S + np.arange(S)[:, None, None]) * K + np.arange(K)[None, :, None]
    item_no = item_no.reshape(P, K * B)
    difference = 0.5 * (np.eye(P, dtype=f32) - np.eye(P, k=1, dtype=f32))
    difference[P - 1, 0] = 0.5
    head_of = np.zeros((2, P, H), f32)
    for h in range(H):
        head_of[h // 4, 32 * (h % 4):32 * (h % 4) + DH, h] = 1.0
    b1 = a["L0_ffn_se_b1"].reshape(-1, P).T
    re_b1 = a["L0_ffn_re_b1"].reshape(E, F // P, P).transpose(2, 0, 1)
    columns = np.concatenate([a["L0_tok_b"][:, None], a["L0_tok_gamma"][:, None], a["L0_tok_beta"][:, None],
                              padded_heads(a["L0_attn_bk"]).reshape(2, P).T, b1, a["L0_attn_bv"][:, None]], axis=1)
    wide = np.concatenate([padded_heads(a["L0_attn_Wk"].T), a["L0_attn_Wq"].T, a["L0_attn_Wv"].T, a["L0_attn_Wo"].T,
                           a["L0_ffn_gate_w"].T, np.eye(P, dtype=f32),
                           head_of.transpose(1, 0, 2).reshape(P, 2 * H),
                           -np.tril(np.ones((P, P), f32)), np.ones((P, P), f32),
                           np.broadcast_to(np.tril(np.ones((E, E), f32), -1).reshape(1, -1), (P, E * E)),
                           np.broadcast_to(a["L0_attn_bq"], (P, C)),
                           np.broadcast_to(np.arange(NT, dtype=f32), (P, NT)), item_no,
                           1 + K * B * S + P * np.arange(NT, dtype=f32)[None, :] + np.arange(P, dtype=f32)[:, None],
                           difference],
                          axis=1)
    rows = np.concatenate([a["L0_attn_bo"], np.ones(P, f32)])[None, :]
    arrays = {"xT": a["x"].transpose(2, 0, 1), "tok_w": a["L0_tok_W"].T, "columns": columns, "wide": wide,
              "rows": rows, "re_w1": a["L0_ffn_re_w1"], "re_w2": a["L0_ffn_re_w2"], "se_w1": a["L0_ffn_se_w1"],
              "se_w2": a["L0_ffn_se_w2"], "re_b2": a["L0_ffn_re_b2"], "se_b2": a["L0_ffn_se_b2"], "re_b1": re_b1}
    arrays = {k: np.ascontiguousarray(v) for k, v in arrays.items()}

    nc = bacc.Bacc("TRN2", target_bir_lowering=False, num_devices=1)
    args = [nc.dram_tensor(k, v.shape, mb.dt.from_np(v.dtype), kind="ExternalInput").ap() for k, v in arrays.items()]
    args.append(nc.dram_tensor("y", (B, S, C), mb.dt.float32, kind="ExternalOutput").ap())
    build(nc, *args)
    return run_bass_kernel_spmd(nc, [arrays], core_ids=[0]).results[0]["y"]
```
